# Optimizing a Trainium2 kernel written in Bass

```python
import numpy as np
import jax
import jax.numpy as jnp

def _softmax(x, axis=-1):
    return jax.nn.softmax(x, axis=axis)

def _gelu(x):
    return jax.nn.gelu(x, approximate=True)

def _silu(x):
    return jax.nn.silu(x)

def _sigmoid(x):
    return jax.nn.sigmoid(x)

def _layernorm(x, axis=-1, eps=1e-05):
    m = jnp.mean(x, axis=axis, keepdims=True)
    v = jnp.var(x, axis=axis, keepdims=True)
    return (x - m) / jnp.sqrt(v + eps)

def _scatter_add(tgt, idx, src, axis=0):
    return tgt.at[idx].add(src)

def _segment_sum(src, seg, n):
    return jax.ops.segment_sum(src, seg, n)
kernel_name = 'mk_adj_ffn_d1_adj_r2_46baad'

def setup_inputs(seed: int=0):
    np.random.seed(seed)
    _w = jnp.asarray

    def _rec_inputs():
        import jax
        import jax.numpy as jnp
        _gk = jax.random.key(seed)
        x = -2.603e-05 + 0.05003 * jax.random.normal(jax.random.fold_in(_gk, 1), (4096, 128), jnp.float32)
        _a = jax.random.bernoulli(jax.random.fold_in(_gk, 2), 0.000976562, (4096, 4096))
        _a = jnp.logical_or(_a, jnp.swapaxes(_a, -1, -2))
        _a = jnp.logical_or(_a, jnp.eye(4096, dtype=bool))
        _af = _a.astype(jnp.float32)
        _af = _af / jnp.maximum(_af.sum(-1, keepdims=True), 1.0)
        adj = _af
        return (x, adj)
    x, adj = _rec_inputs()

    def _L0_gnn_setup():
        import jax, jax.numpy as jnp
        import numpy as np
        MIN_NORM = 1e-15
        BALL_EPS = 1e-05
        C_IN = 1.0
        C_OUT = 1.0

        def _artanh(x):
            x = jnp.clip(x, -1.0 + 1e-07, 1.0 - 1e-07)
            return 0.5 * (jnp.log1p(x) - jnp.log1p(-x))

        def _norm(x):
            return jnp.maximum(jnp.linalg.norm(x, axis=-1, keepdims=True), MIN_NORM)

        def proj(x, c):
            norm = _norm(x)
            maxnorm = (1.0 - BALL_EPS) / jnp.sqrt(c)
            return jnp.where(norm > maxnorm, x / norm * maxnorm, x)

        def expmap0(u, c):
            sc = jnp.sqrt(c)
            un = _norm(u)
            return jnp.tanh(sc * un) * u / (sc * un)

        def logmap0(p, c):
            sc = jnp.sqrt(c)
            pn = _norm(p)
            return _artanh(sc * pn) * p / (sc * pn)

        def mobius_matvec(m, x, c):
            sc = jnp.sqrt(c)
            xn = _norm(x)
            mx = x @ m.T
            mxn = _norm(mx)
            res = jnp.tanh(mxn / xn * _artanh(sc * xn)) * mx / (mxn * sc)
            zero_row = jnp.all(mx == 0, axis=-1, keepdims=True)
            return jnp.where(zero_row, jnp.zeros((), dtype=res.dtype), res)

        def mobius_add(x, y, c):
            x2 = jnp.sum(x * x, axis=-1, keepdims=True)
            y2 = jnp.sum(y * y, axis=-1, keepdims=True)
            xy = jnp.sum(x * y, axis=-1, keepdims=True)
            num = (1.0 + 2.0 * c * xy + c * y2) * x + (1.0 - c * x2) * y
            denom = 1.0 + 2.0 * c * xy + c * c * x2 * y2
            return num / jnp.maximum(denom, MIN_NORM)
        key = jax.random.key(seed)
        k1, k2, k3, k4 = jax.random.split(key, 4)
        N, D_IN, D_OUT = (4096, 128, 128)
        x = proj(0.05 * jax.random.normal(k1, (N, D_IN), dtype=jnp.float32), C_IN)
        adj = jax.random.uniform(k2, (N, N), dtype=jnp.float32)
        adj = adj / jnp.sum(adj, axis=1, keepdims=True)
        bound = np.sqrt(2.0) * np.sqrt(6.0 / (D_IN + D_OUT))
        weight = jax.random.uniform(k3, (D_OUT, D_IN), dtype=jnp.float32, minval=-bound, maxval=bound)
        bias = 0.01 * jax.random.normal(k4, (D_OUT,), dtype=jnp.float32)
        return {'x': x, 'adj': adj, 'weight': weight, 'bias': bias}
    _L0_gnn_all = _L0_gnn_setup()
    _L0_gnn_in = {k: v for k, v in _L0_gnn_all.items() if k in ('weight', 'bias')}
    del _L0_gnn_all

    def _L0_ffn_setup():
        import jax, jax.numpy as jnp
        import numpy as np
        B, T, IN_DIM = (64, 128, 128)
        HID, OUT_DIM = (256, 128)
        N_LAYERS, N_EXPERTS, N_SHARED = (2, 16, 1)
        key = jax.random.key(seed)
        ks = jax.random.split(key, 10)
        s = 0.02
        x = jax.random.normal(ks[0], (B, T, IN_DIM), dtype=jnp.float32)
        route_id = jax.random.randint(ks[1], (B,), 0, N_EXPERTS)
        Wi = jax.random.normal(ks[2], (HID, IN_DIM), dtype=jnp.float32) * s
        bi = jnp.zeros((HID,), dtype=jnp.float32)
        Wr = jax.random.normal(ks[3], (N_LAYERS, N_EXPERTS, HID, HID), dtype=jnp.float32) * s
        br = jax.random.normal(ks[4], (N_LAYERS, N_EXPERTS, HID), dtype=jnp.float32) * s
        Ws = jax.random.normal(ks[5], (N_LAYERS, N_SHARED, HID, HID), dtype=jnp.float32) * s
        bs = jax.random.normal(ks[6], (N_LAYERS, N_SHARED, HID), dtype=jnp.float32) * s
        Wo = jax.random.normal(ks[7], (OUT_DIM, HID), dtype=jnp.float32) * s
        bo = jnp.zeros((OUT_DIM,), dtype=jnp.float32)
        return {'x': x, 'route_id': route_id, 'Wi': Wi, 'bi': bi, 'Wr': Wr, 'br': br, 'Ws': Ws, 'bs': bs, 'Wo': Wo, 'bo': bo}
    _L0_ffn_all = _L0_ffn_setup()
    _L0_ffn_in = {k: v for k, v in _L0_ffn_all.items() if k in ('route_id', 'Wi', 'bi', 'Wr', 'br', 'Ws', 'bs', 'Wo', 'bo')}
    del _L0_ffn_all
    return {'x': x, 'adj': adj, 'L0_gnn_weight': _L0_gnn_in['weight'], 'L0_gnn_bias': _L0_gnn_in['bias'], 'L0_ffn_route_id': _L0_ffn_in['route_id'], 'L0_ffn_Wi': _L0_ffn_in['Wi'], 'L0_ffn_bi': _L0_ffn_in['bi'], 'L0_ffn_Wr': _L0_ffn_in['Wr'], 'L0_ffn_br': _L0_ffn_in['br'], 'L0_ffn_Ws': _L0_ffn_in['Ws'], 'L0_ffn_bs': _L0_ffn_in['bs'], 'L0_ffn_Wo': _L0_ffn_in['Wo'], 'L0_ffn_bo': _L0_ffn_in['bo']}

def reference(x, adj, L0_gnn_weight, L0_gnn_bias, L0_ffn_route_id, L0_ffn_Wi, L0_ffn_bi, L0_ffn_Wr, L0_ffn_br, L0_ffn_Ws, L0_ffn_bs, L0_ffn_Wo, L0_ffn_bo):
    import jax
    import jax.numpy as jnp

    def _L0_gnn_ref(x, adj, weight, bias):
        import jax, jax.numpy as jnp
        import numpy as np
        MIN_NORM = 1e-15
        BALL_EPS = 1e-05
        C_IN = 1.0
        C_OUT = 1.0

        def _artanh(x):
            x = jnp.clip(x, -1.0 + 1e-07, 1.0 - 1e-07)
            return 0.5 * (jnp.log1p(x) - jnp.log1p(-x))

        def _norm(x):
            return jnp.maximum(jnp.linalg.norm(x, axis=-1, keepdims=True), MIN_NORM)

        def proj(x, c):
            norm = _norm(x)
            maxnorm = (1.0 - BALL_EPS) / jnp.sqrt(c)
            return jnp.where(norm > maxnorm, x / norm * maxnorm, x)

        def expmap0(u, c):
            sc = jnp.sqrt(c)
            un = _norm(u)
            return jnp.tanh(sc * un) * u / (sc * un)

        def logmap0(p, c):
            sc = jnp.sqrt(c)
            pn = _norm(p)
            return _artanh(sc * pn) * p / (sc * pn)

        def mobius_matvec(m, x, c):
            sc = jnp.sqrt(c)
            xn = _norm(x)
            mx = x @ m.T
            mxn = _norm(mx)
            res = jnp.tanh(mxn / xn * _artanh(sc * xn)) * mx / (mxn * sc)
            zero_row = jnp.all(mx == 0, axis=-1, keepdims=True)
            return jnp.where(zero_row, jnp.zeros((), dtype=res.dtype), res)

        def mobius_add(x, y, c):
            x2 = jnp.sum(x * x, axis=-1, keepdims=True)
            y2 = jnp.sum(y * y, axis=-1, keepdims=True)
            xy = jnp.sum(x * y, axis=-1, keepdims=True)
            num = (1.0 + 2.0 * c * xy + c * y2) * x + (1.0 - c * x2) * y
            denom = 1.0 + 2.0 * c * xy + c * c * x2 * y2
            return num / jnp.maximum(denom, MIN_NORM)
        h = proj(mobius_matvec(weight, x, C_IN), C_IN)
        hyp_bias = proj(expmap0(bias[None, :], C_IN), C_IN)
        h = proj(mobius_add(h, hyp_bias, C_IN), C_IN)
        x_tangent = logmap0(h, C_IN)
        support_t = adj @ x_tangent
        h = proj(expmap0(support_t, C_IN), C_IN)
        xt = jax.nn.relu(logmap0(h, C_IN))
        return proj(expmap0(xt, C_OUT), C_OUT)

    def _L0_ffn_ref(x, route_id, Wi, bi, Wr, br, Ws, bs, Wo, bo):
        import jax, jax.numpy as jnp
        import numpy as np
        B, T, IN_DIM = (64, 128, 128)
        HID, OUT_DIM = (256, 128)
        N_LAYERS, N_EXPERTS, N_SHARED = (2, 16, 1)
        flat = x.reshape(-1, x.shape[-1])
        n_tok = flat.shape[0]
        route = jnp.repeat(route_id, n_tok // route_id.shape[0])
        h = jax.nn.relu(flat @ Wi.T + bi)
        n_layers, n_experts = (Wr.shape[0], Wr.shape[1])
        for l in range(n_layers):
            shared = (jnp.einsum('nd,shd->snh', h, Ws[l]) + bs[l][:, None, :]).mean(axis=0)
            routed = jnp.zeros_like(h)
            for e in range(n_experts):
                ye = h @ Wr[l, e].T + br[l, e]
                routed = routed + jnp.where((route == e)[:, None], ye, 0.0)
            h = jax.nn.relu(shared + routed + h)
        out = h @ Wo.T + bo
        return out.reshape(*x.shape[:-1], out.shape[-1])
    x = x + _L0_gnn_ref(_layernorm(x, axis=-1), adj, L0_gnn_weight, L0_gnn_bias)
    x = x + _L0_ffn_ref(_layernorm(x, axis=-1)[None], L0_ffn_route_id, L0_ffn_Wi, L0_ffn_bi, L0_ffn_Wr, L0_ffn_br, L0_ffn_Ws, L0_ffn_bs, L0_ffn_Wo, L0_ffn_bo)[0]
    return x

_drawn_inputs = setup_inputs


def setup_inputs(seed=0):
    import zlib

    import numpy as np

    out = dict(_drawn_inputs(seed))
    spreads = {'L0_ffn_bi': (0.0, 0.1), 'L0_ffn_bo': (0.0, 0.1)}
    factors = {}
    for name, (base, spread) in spreads.items():
        noise = np.random.default_rng([zlib.crc32(name.encode()), seed]).standard_normal(out[name].shape)
        drawn = base * np.exp(spread * noise) if base else spread * noise
        out[name] = jnp.asarray(drawn.astype(out[name].dtype))
    for name, factor in factors.items():
        out[name] = (out[name] * factor).astype(out[name].dtype)
    return out
```

```python
from contextlib import ExitStack

import numpy as np

import concourse.bass as bass
from concourse import mybir

F32 = mybir.dt.float32
F32R = mybir.dt.float32r
I32 = mybir.dt.int32
ALU = mybir.AluOpType
ACT = mybir.ActivationFunctionType
AX_X = mybir.AxisListType.X

P = 128
N = 4096
D = 128
HID = 256
KT = N // P
ROWS = 512
BLOCKS = N // ROWS
TILES = ROWS // P
CK = 4
CHUNKS = KT // CK
CW = CK * ROWS
RAW = 4
SUBS = 2
PART = 4
SW = CW // SUBS
SK = CK // SUBS
HALVES = CHUNKS * SUBS

LAYERS, EXPERTS = 2, 16
E1 = EXPERTS + 1
GROUPS = 64
GR = N // GROUPS
SLOTS = (GROUPS + E1) // 2
KH = HID // P

MIN_NORM = 1e-15
MIN_SQ = 1e-30
MAX_NORM = float(np.float32(1.0 - 1e-5))
CLIP = float(np.float32(1.0 - 1e-7))
ATANH_MAX = float(np.arctanh(np.float64(np.float32(1.0 - 1e-5))))
LN_EPS = 1e-5
ATANH_SERIES = [1.0 / 13, 1.0 / 11, 1.0 / 9, 1.0 / 7, 1.0 / 5, 1.0 / 3]

LOAD, STATS, NORM, T0, WI, L0, T1, L1, T2, WO = -4, -2, -1, 0, 1, 2, 3, 4, 5, 6
HEAD = range(LOAD, 8)
BODY = (8, SLOTS + LOAD)
POST_AT = [1, 4, 7]
DVE_POST_AT = [4, 6, 7]
TAIL = range(SLOTS + LOAD, SLOTS + WO)


def build(nc, x, adj_t, w, w_t, bias, route, wi_t, bi, wr_t, ws_t, b_t, wo_t, bo, x2_dram, out):
    with ExitStack() as ctx:
        def sb(name, shape, dt=F32):
            return ctx.enter_context(nc.sbuf_tensor(name, shape, dt))

        def sem(name):
            return ctx.enter_context(nc.semaphore(name))

        bank = [ctx.enter_context(nc.psum_tensor(f"bank{i}", [P, 512], F32)) for i in range(8)]

        xm = sb("xm", [P, KT, D])
        xt_hi = sb("xt_hi", [P, KT, D], F32R)
        xt_lo = sb("xt_lo", [P, KT, D], F32R)
        raw = sb("raw", [P, RAW * CW])
        adj_hi = sb("adj_hi", [P, PART, SW], F32R)
        adj_lo = sb("adj_lo", [P, PART, SW], F32R)
        weff = sb("weff", [P, LAYERS * KH, E1, HID])
        bt = sb("bt", [P, LAYERS * KH, E1])
        wi_sb = sb("wi_sb", [P, HID])
        bi_sb = sb("bi_sb", [P, KH])
        wo_sb = sb("wo_sb", [P, KH, D])
        bo_bc = sb("bo_bc", [P, D])
        w_sb = sb("w_sb", [P, D])
        wt_sb = sb("wt_sb", [P, D])
        b_col = sb("b_col", [P, 1])
        b_bc = sb("b_bc", [P, D])
        ident = sb("ident", [P, P])
        ones = sb("ones", [P, P])
        work = sb("work", [P, 2, 512])
        sq = sb("sq", [P, 2, 512])
        rl = sb("rl", [P, 512])
        xr = sb("xr", [P, 2, TILES, D])
        st6 = sb("st6", [P, KT, 6])
        mv = sb("mv", [P, KT, 2])
        wb = sb("wb", [P, 1])
        sc = sb("sc", [P, 22, KT])
        row = [sc[:, n, :] for n in range(22)]
        bsc = sb("bsc", [P, 8])
        tmp_i = sb("tmp_i", [P, 2 * KT], I32)
        tmp_f = sb("tmp_f", [P, 2 * KT])
        f_expo = sb("f_expo", [P, 1])
        ga = sb("ga", [P, 16, TILES])
        r_int = sb("r_int", [GROUPS, GROUPS + 1], I32)
        r_f = sb("r_f", [GROUPS, GROUPS + 1])
        valid = sb("valid", [GROUPS, GROUPS + 1])
        later = rl[0:GROUPS, 0:GROUPS]
        earlier = rl[0:GROUPS, GROUPS:2 * GROUPS]
        rt = [rl[0:GROUPS, (2 + n) * GROUPS:(3 + n) * GROUPS] for n in range(5)]
        rc = sb("rc", [GROUPS, 8])
        rci = sb("rci", [GROUPS, 2], I32)
        iota_f = sb("iota_f", [GROUPS, SLOTS])
        lead = sb("lead", [GROUPS, 2, SLOTS])
        mrow = sb("mrow", [1, 8, SLOTS])
        mint = sb("mint", [1, 5, SLOTS], I32)
        f_mv = sb("f_mv", [P, 2, 10])
        f_rs = sb("f_rs", [P, 2, 1])
        flat = xm[:, :, :].rearrange("p t d -> p (t d)")

        def ring(at, width):
            return [flat[:, at + n * width:at + (n + 1) * width] for n in range(2)]

        f_xn, f_xt, f_o = ring(0, D), ring(2 * D, P), ring(4 * D, D)
        f_h0, f_u0, f_h1, f_u1, f_h2 = (ring(6 * D + n * 2 * HID, HID) for n in range(5))

        x_loaded = [sem(f"x_loaded{n}") for n in range(4)]
        wload = sem("wload")
        route_loaded = sem("route_loaded")
        wr_loaded = sem("wr_loaded")
        pool_step = sem("pool_step")
        consts_made = sem("consts_made")
        dve_step = sem("dve_step")
        act_step = sem("act_step")
        even_ready = sem("even_ready")
        slot_mm = sem("slot_mm")
        lead_ready = sem("lead_ready")
        tables_mm = sem("tables_mm")
        meta_ready = sem("meta_ready")
        bsq_ready = sem("bsq_ready")
        bias_mm = sem("bias_mm")
        wb_ready = sem("wb_ready")
        xn_ready = sem("xn_ready")
        xnt_in_psum = sem("xnt_in_psum")
        xnt_copied = sem("xnt_copied")
        mx_in_psum = sem("mx_in_psum")
        xb_in_psum = sem("xb_in_psum")
        mx_copied = sem("mx_copied")
        mx_squared = sem("mx_squared")
        sq_used = sem("sq_used")
        fn_asked = sem("fn_asked")
        fn_done = sem("fn_done")
        gains_ready = sem("gains_ready")
        mx_scaled = sem("mx_scaled")
        xt_sum = sem("xt_sum")
        xt_hi_made = sem("xt_hi_made")
        xt_ready = sem("xt_ready")
        adj_loaded = [sem(f"adj_loaded{n}") for n in range(RAW)]
        hi_made = sem("hi_made")
        lo_made = sem("lo_made")
        half_used = sem("half_used")
        support_ready = sem("support_ready")
        support_copied = sem("support_copied")
        rows_ready = sem("rows_ready")
        rows_squared = sem("rows_squared")
        relu_made = sem("relu_made")
        relu_squared = sem("relu_squared")
        sums_read = sem("sums_read")
        tanh_asked = sem("tanh_asked")
        tanh_made = sem("tanh_made")
        ga_step = sem("ga_step")
        xr_loaded = [sem(f"xr_loaded{n}") for n in range(2)]
        x2_ready = sem("x2_ready")
        x2_stored = [sem(f"x2_stored{n}") for n in range(2)]
        weff_made = sem("weff_made")
        slot_loaded = [sem(f"slot_loaded{n}") for n in range(2)]
        f_stats = sem("f_stats")
        f_mean = sem("f_mean")
        f_var = sem("f_var")
        f_rstd = sem("f_rstd")
        f_xn_ready = sem("f_xn_ready")
        t0_done = sem("t0_done")
        xt_copied = sem("xt_copied")
        wi_done = sem("wi_done")
        h0_made = sem("h0_made")
        l0_done = sem("l0_done")
        u0_made = sem("u0_made")
        t1_done = sem("t1_done")
        h1_made = sem("h1_made")
        l1_done = sem("l1_done")
        u1_made = sem("u1_made")
        t2_done = sem("t2_done")
        h2_made = sem("h2_made")
        wo_done = sem("wo_done")
        o_sum = sem("o_sum")
        o_made = sem("o_made")
        o_stored = [sem(f"o_stored{n}") for n in range(2)]

        def wait(eng, semaphore, value):
            if isinstance(value, int) and value <= 0:
                return
            eng.wait_ge(semaphore, value)

        def blocks(eng, block_step):
            block_step(0, 0)
            block_step(1, 1)
            with eng.Fori(1, BLOCKS // 2) as pair:
                block_step(pair * 2, 0)
                block_step(pair * 2 + 1, 1)

        def pipeline(eng, iteration):
            for i in HEAD:
                iteration(i, i % 2)
            with eng.Fori(BODY[0] // 2, BODY[1] // 2) as pair:
                iteration(pair * 2, 0)
                iteration(pair * 2 + 1, 1)
            for i in TAIL:
                iteration(i, i % 2)

        def live(slot):
            return not isinstance(slot, int) or 0 <= slot < SLOTS

        raw_c = [raw[:, r * CW:(r + 1) * CW] for r in range(RAW)]
        WLOADS = 10
        QUADS = KT // 4

        block = ctx.enter_context(nc.Block())

        @block.sync
        def _(sp):
            sp.dma_start(r_int[:, 0:GROUPS], route.rearrange("(a n) -> a n", a=1).to_broadcast([GROUPS, GROUPS])).then_inc(route_loaded, 16)
            sp.dma_start(r_int[:, GROUPS:GROUPS + 1], route.rearrange("(n a) -> n a", a=1)).then_inc(route_loaded, 16)
            for n in range(4):
                sp.dma_start(xm[:, n * 8:(n + 1) * 8, :],
                             x.rearrange("(p t) d -> p t d", p=P)[:, n * 8:(n + 1) * 8, :]).then_inc(x_loaded[n], 16)
            sp.dma_start(w_sb[:, :], w).then_inc(wload, 16)
            sp.dma_start(wt_sb[:, :], w_t).then_inc(wload, 16)
            sp.dma_start(b_col[:, :], bias.rearrange("(p a) -> p a", a=1)).then_inc(wload, 16)
            sp.dma_start(b_bc[:, :], bias.rearrange("(a n) -> a n", a=1).to_broadcast([P, D])).then_inc(wload, 16)
            sp.dma_start(wi_sb[:, :], wi_t).then_inc(wload, 16)
            sp.dma_start(bi_sb[:, :], bi).then_inc(wload, 16)
            sp.dma_start(wo_sb[:, :, :], wo_t).then_inc(wload, 16)
            sp.dma_start(bo_bc[:, :], bo.rearrange("(a n) -> a n", a=1).to_broadcast([P, D])).then_inc(wload, 16)
            sp.dma_start(weff[:, :, EXPERTS, :], ws_t).then_inc(wload, 16)
            sp.dma_start(bt[:, :, :], b_t).then_inc(wload, 16)
            for c in range(RAW):
                sp.dma_start(raw_c[c], adj_t[0, :, c * CW:(c + 1) * CW]).then_inc(adj_loaded[c], 16)
            for lk in range(LAYERS * KH):
                sp.dma_start(weff[:, lk, 0:EXPERTS, :], wr_t[:, lk, :, :]).then_inc(wr_loaded, 16)

            def load_block(b, par):
                for c in range(CHUNKS):
                    if isinstance(b, int) and b * CHUNKS + c < RAW:
                        continue
                    sp.wait_ge(lo_made, (b * CHUNKS + c - RAW + 1) * SUBS)
                    sp.dma_start(raw_c[c % RAW], adj_t[bass.ds(b, 1), :, c * CW:(c + 1) * CW].rearrange("a p n -> (a p) n")
                                 ).then_inc(adj_loaded[c % RAW], 16)
            blocks(sp, load_block)

            sp.wait_ge(meta_ready, 1)

            def iteration(i, par):
                s = i - WO
                if live(s):
                    sp.wait_ge(o_made, s + 1)
                    for g in range(2):
                        dst = sp.value_load(mint[0:1, 3 + g, bass.ds(s, 1)], min_val=0, max_val=GROUPS + 2 * SLOTS - 1)
                        sp.dma_start(out[bass.ds(dst * GR, GR), :],
                                     f_o[par][g * GR:(g + 1) * GR, :]).then_inc(o_stored[par], 16)
            pipeline(sp, iteration)
            for par in range(2):
                sp.wait_ge(o_stored[par], SLOTS // 2 * 32)

        @block.gpsimd
        def _(pool):
            steps = 0
            for dst, val in ((ident[:, :], 0.0), (ones[:, :], 1.0), (later, 1.0), (earlier, 1.0),
                             (f_expo[:, :], -0.5)):
                nc.gpsimd.memset(dst, val).then_inc(pool_step, 1)
                steps += 1
            nc.gpsimd.iota(iota_f[:, :], pattern=[[1, SLOTS]], base=0, channel_multiplier=0,
                           allow_small_or_imprecise_dtypes=True).then_inc(pool_step, 1)
            nc.gpsimd.iota(rc[:, 7:8], pattern=[[0, 1]], base=0, channel_multiplier=1,
                           allow_small_or_imprecise_dtypes=True).then_inc(pool_step, 1)
            steps += 2
            pool.wait_ge(pool_step, steps)
            nc.gpsimd.affine_select(out=ident[:, :], in_=ident[:, :], compare_op=ALU.not_equal, fill=1.0, base=0,
                                    pattern=[[-1, P]], channel_multiplier=1).then_inc(consts_made, 1)
            nc.gpsimd.affine_select(out=later, in_=later, compare_op=ALU.is_gt, fill=0.0, base=0,
                                    pattern=[[1, GROUPS]], channel_multiplier=-1).then_inc(consts_made, 1)
            nc.gpsimd.affine_select(out=earlier, in_=earlier, compare_op=ALU.is_gt, fill=0.0, base=0,
                                    pattern=[[-1, GROUPS]], channel_multiplier=1).then_inc(consts_made, 1)

            pool.wait_ge(consts_made, 3)
            pool.wait_ge(wload, 16 * WLOADS)
            pool.wait_ge(wr_loaded, 16 * LAYERS * KH)
            for lk in range(LAYERS * KH):
                diag = weff[:, lk, EXPERTS, (lk % KH) * P:(lk % KH + 1) * P]
                nc.gpsimd.tensor_tensor(diag, diag, ident[:, :], ALU.add).then_inc(pool_step, 1)
                pool.wait_ge(pool_step, steps + lk + 1)
                nc.gpsimd.tensor_tensor(weff[:, lk, 0:EXPERTS, :], weff[:, lk, 0:EXPERTS, :],
                                        weff[:, lk, EXPERTS:E1, :].to_broadcast([P, EXPERTS, HID]), ALU.add).then_inc(weff_made, 1)
            nc.gpsimd.tensor_tensor(bt[:, :, 0:EXPERTS], bt[:, :, 0:EXPERTS],
                                    bt[:, :, EXPERTS:E1].to_broadcast([P, LAYERS * KH, EXPERTS]), ALU.add).then_inc(weff_made, 1)

            pool.dma_start(xr[:, 0, :, :], x[0:ROWS, :].rearrange("(q p) d -> p q d", p=P)).then_inc(xr_loaded[0], 16)

            def block_step(b, par, last=False):
                if not last:
                    wait(pool, x2_stored[1 - par], 16 * (b // 2 + par) if isinstance(b, int) else (b + par) * 8)
                    pool.dma_start(xr[:, 1 - par, :, :], x[bass.ds(b * ROWS + ROWS, ROWS), :].rearrange("(q p) d -> p q d", p=P)
                                   ).then_inc(xr_loaded[1 - par], 16)
                pool.wait_ge(x2_ready, b * TILES + TILES)
                pool.dma_start(x2_dram[bass.ds(b * ROWS, ROWS), :].rearrange("(q p) d -> p q d", p=P),
                               xr[:, par, :, :]).then_inc(x2_stored[par], 16)

            block_step(0, 0)
            block_step(1, 1)
            with pool.Fori(1, BLOCKS // 2 - 1) as pair:
                block_step(pair * 2, 0)
                block_step(pair * 2 + 1, 1)
            block_step(BLOCKS - 2, 0)
            block_step(BLOCKS - 1, 1, last=True)

            for par in range(2):
                pool.wait_ge(x2_stored[par], BLOCKS // 2 * 16)
            pool.wait_ge(lo_made, BLOCKS * HALVES)
            pool.wait_ge(meta_ready, 1)

            def iteration(i, par):
                s = i - LOAD
                if live(s):
                    wait(pool, slot_loaded[par], (s - par) * 16)
                    for g in range(2):
                        src = pool.value_load(mint[0:1, g, bass.ds(s, 1)], min_val=0, max_val=GROUPS - 1)
                        pool.dma_start(raw[g * GR:(g + 1) * GR, bass.ds(s * D, D)],
                                     x2_dram[bass.ds(src * GR, GR), :]).then_inc(slot_loaded[par], 16)
                s, q = i - STATS, par
                if live(s):
                    pool.wait_ge(f_var, s + 1)
                    nc.gpsimd.tensor_tensor(f_rs[:, q, :], f_mv[:, q, 8:9], f_expo[:, :], ALU.pow).then_inc(f_rstd, 1)
            pipeline(pool, iteration)

        @block.scalar
        def _(act):
            act.wait_ge(fn_asked, 1)
            nc.scalar.activation(bsc[:, 3:4], bsc[:, 1:2], ACT.Tanh).then_inc(fn_done, 1)

            def copy_xnt(g):
                act.wait_ge(xnt_in_psum, g + 1)
                if g >= 2:
                    act.wait_ge(mx_in_psum, g - 1)
                nc.scalar.activation(work[:, g % 2, :], bank[g % 2][:, :], ACT.Copy).then_inc(xnt_copied, 1)

            copy_xnt(0)
            for g in range(QUADS):
                if g + 1 < QUADS:
                    copy_xnt(g + 1)
                act.wait_ge(mx_in_psum, g + 1)
                mx = bank[2 + g % 2][:, :]
                nc.scalar.activation(xm[:, 4 * g:4 * g + 4, :].rearrange("p t d -> p (t d)"), mx, ACT.Copy).then_inc(mx_copied, 1)
                if g >= 2:
                    act.wait_ge(sq_used, g - 1)
                nc.scalar.activation(sq[:, g % 2, :], mx, ACT.Square).then_inc(mx_squared, 1)

            def logs(asked):
                act.wait_ge(fn_asked, asked)
                nc.scalar.activation(row[12], row[10], ACT.Ln, bias=1.0).then_inc(fn_done, 1)
                nc.scalar.activation(row[13], row[10], ACT.Ln, bias=1.0, scale=-1.0).then_inc(fn_done, 1)

            logs(2)
            act.wait_ge(fn_asked, 3)
            nc.scalar.activation(row[15], row[14], ACT.Tanh).then_inc(fn_done, 1)
            logs(4)
            act.wait_ge(gains_ready, 1)
            def split_hi(b, c):
                act.wait_ge(adj_loaded[c % RAW], b * (CHUNKS // RAW * 16) + (c // RAW + 1) * 16)
                for h in range(SUBS):
                    wait(act, half_used, b * HALVES + c * SUBS + h - PART + 1)
                    nc.scalar.activation(adj_hi[:, (c * SUBS + h) % PART, :], raw_c[c % RAW][:, h * SW:(h + 1) * SW],
                                         ACT.Copy).then_inc(hi_made, 1)

            def scale_quad(g):
                for t in range(4 * g, 4 * g + 4):
                    mm = nc.scalar.activation(xm[:, t, :], xm[:, t, :], ACT.Copy, scale=row[20][:, t:t + 1])
                mm.then_inc(mx_scaled, 1)

            def hi_quad(g):
                act.wait_ge(xt_sum, g + 1)
                nc.scalar.activation(xt_hi[:, 4 * g:4 * g + 4, :], xm[:, 4 * g:4 * g + 4, :], ACT.Copy).then_inc(xt_hi_made, 1)

            def post(b, par, step):
                rows = bank[2 + par][:, :]
                if step == 0:
                    act.wait_ge(support_ready, b + 1)
                    nc.scalar.activation(work[:, par, :], bank[par][:, :], ACT.Copy).then_inc(support_copied, 1)
                if step == 1:
                    act.wait_ge(rows_ready, b + 1)
                    wait(act, sums_read, 2 * b)
                    nc.scalar.activation(sq[:, 0, :], rows, ACT.Square).then_inc(rows_squared, 1)
                    wait(act, x2_ready, b * TILES)
                    nc.scalar.activation(rl[:, :], rows, ACT.Relu).then_inc(relu_made, 1)
                    act.wait_ge(relu_made, b + 1)
                    nc.scalar.activation(sq[:, 1, :], rl[:, :], ACT.Square).then_inc(relu_squared, 1)
                if step == 2:
                    act.wait_ge(tanh_asked, b + 1)
                    nc.scalar.activation(ga[:, 11, :], ga[:, 10, :], ACT.Tanh).then_inc(tanh_made, 1)

            def block_step(b, par):
                first = isinstance(b, int) and b == 0
                for c in range(CHUNKS):
                    if first:
                        scale_quad(c)
                        if c >= 1:
                            hi_quad(c - 1)
                        if c == CHUNKS - 1:
                            hi_quad(c)
                    split_hi(b, c)
                    if not first and c in POST_AT:
                        post(b - 1, 1 - par, POST_AT.index(c))
            blocks(act, block_step)
            for step in range(3):
                post(BLOCKS - 1, 1, step)

            def iteration(i, par):
                s, q = i - L1, par
                if live(s):
                    act.wait_ge(l1_done, s + 1)
                    wait(act, t2_done, s - 1)
                    nc.scalar.activation(f_u1[q], bank[4][:, 0:HID], ACT.Copy).then_inc(u1_made, 1)
                s, q = i - L0, par
                if live(s):
                    act.wait_ge(l0_done, s + 1)
                    wait(act, t1_done, s - 1)
                    nc.scalar.activation(f_u0[q], bank[2][:, 0:HID], ACT.Copy).then_inc(u0_made, 1)
                s, q = i - WI, 1 - par
                if live(s):
                    act.wait_ge(wi_done, s + 1)
                    wait(act, l0_done, s - 1)
                    for k in range(KH):
                        nc.scalar.activation(f_h0[q][:, k * P:(k + 1) * P], bank[1][:, k * P:(k + 1) * P], ACT.Relu,
                                             bias=bi_sb[:, k:k + 1]).then_inc(h0_made, 1)
                s, q = i - T0, par
                if live(s):
                    act.wait_ge(t0_done, s + 1)
                    wait(act, wi_done, s - 1)
                    nc.scalar.activation(f_xt[q], bank[0][:, 0:P], ACT.Copy).then_inc(xt_copied, 1)
            pipeline(act, iteration)

        @block.vector
        def _(dve):
            chain = [0]

            def link(ins):
                chain[0] += 1
                ins.then_inc(dve_step, 1)
                dve.wait_ge(dve_step, chain[0])

            V = nc.vector
            dve.wait_ge(route_loaded, 32)
            link(V.tensor_copy(r_f[:, :], r_int[:, :]))
            link(V.tensor_scalar(valid[:, :], r_f[:, :], 0.0, None, ALU.is_ge))
            link(V.scalar_tensor_tensor(out=valid[:, :], in0=r_f[:, :], scalar=float(EXPERTS - 1), in1=valid[:, :],
                                        op0=ALU.is_le, op1=ALU.mult))
            link(V.scalar_tensor_tensor(out=r_f[:, :], in0=r_f[:, :], scalar=-float(EXPERTS), in1=valid[:, :],
                                        op0=ALU.add, op1=ALU.mult))
            link(V.tensor_scalar(r_f[:, :], r_f[:, :], float(EXPERTS), None, ALU.add))
            own = r_f[:, GROUPS:GROUPS + 1]
            dve.wait_ge(consts_made, 3)
            V.tensor_scalar(rt[1], r_f[:, 0:GROUPS], own, None, ALU.is_gt)
            link(V.tensor_scalar(rt[0], r_f[:, 0:GROUPS], own, None, ALU.is_equal))
            V.tensor_tensor(rt[2], rt[0], later, ALU.mult)
            link(V.tensor_tensor(rt[3], rt[0], earlier, ALU.mult))
            link(V.tensor_reduce(rc[:, 0:1], rt[3], AX_X, ALU.add))
            link(V.tensor_copy(rci[:, 0:1], rc[:, 0:1]))
            link(V.tensor_scalar(rci[:, 1:2], rci[:, 0:1], 1, None, ALU.bitwise_and))
            link(V.tensor_copy(rc[:, 1:2], rci[:, 1:2]))
            link(V.tensor_scalar(rc[:, 2:3], rc[:, 1:2], -1.0, 1.0, ALU.mult, ALU.add))
            V.tensor_tensor(rt[4], rt[1], rt[2], ALU.add).then_inc(even_ready, 1)
            dve.wait_ge(slot_mm, 1)
            link(V.tensor_tensor(rc[:, 3:4], bank[5][0:GROUPS, 0:1], rc[:, 1:2], ALU.subtract))
            V.tensor_scalar(lead[:, 0, :], iota_f[:, :], rc[:, 3:4], rc[:, 2:3], ALU.is_equal, ALU.mult)
            V.tensor_scalar(lead[:, 1, :], iota_f[:, :], rc[:, 3:4], rc[:, 1:2], ALU.is_equal, ALU.mult).then_inc(lead_ready, 1)
            dve.wait_ge(tables_mm, 1)
            link(V.tensor_copy(mrow[0:1, 0:5, :].rearrange("a k s -> a (k s)"), bank[6][0:1, 0:5 * SLOTS]))
            m = [mrow[0:1, k, :] for k in range(8)]
            link(V.tensor_scalar(m[4], m[4], -1.0, 1.0, ALU.mult, ALU.add))
            link(V.tensor_tensor(m[5], m[4], m[0], ALU.mult))
            link(V.tensor_tensor(m[5], m[5], m[3], ALU.add))
            link(V.tensor_scalar(m[1], m[1], -1.0, 1.0, ALU.mult, ALU.add))
            link(V.scalar_tensor_tensor(out=m[6], in0=iota_f[0:1, :], scalar=float(GROUPS), in1=m[1],
                                        op0=ALU.add, op1=ALU.mult))
            link(V.tensor_tensor(m[6], m[6], m[0], ALU.add))
            link(V.scalar_tensor_tensor(out=m[7], in0=iota_f[0:1, :], scalar=float(GROUPS + SLOTS), in1=m[4],
                                        op0=ALU.add, op1=ALU.mult))
            link(V.tensor_tensor(m[7], m[7], m[3], ALU.add))
            for k, src in enumerate((0, 5, 2, 6, 7)):
                ins = V.tensor_copy(mint[0:1, k, :], m[src])
            link(ins)
            V.tensor_copy(mrow[0:1, 0, 0:1], mrow[0:1, 1, 0:1]).then_inc(meta_ready, 1)

            def inverse_root(dst, src, width, chained):
                ti, tf = tmp_i[:, 0:width], tmp_f[:, 0:width]
                chained(V.tensor_scalar(ti, src.bitcast(I32), 1, None, ALU.logical_shift_right))
                chained(V.tensor_scalar(dst.bitcast(I32), ti, -1.0, float(0x5F3759DF), ALU.mult, ALU.add))
                for _ in range(3):
                    chained(V.tensor_tensor(tf, dst, dst, ALU.mult))
                    chained(V.scalar_tensor_tensor(out=tf, in0=tf, scalar=-0.5, in1=src, op0=ALU.mult, op1=ALU.mult))
                    chained(V.scalar_tensor_tensor(out=dst, in0=tf, scalar=1.5, in1=dst, op0=ALU.add, op1=ALU.mult))

            dve.wait_ge(wload, 16 * WLOADS)
            V.tensor_tensor(bsc[:, 0:1], b_col[:, :], b_col[:, :], ALU.mult).then_inc(bsq_ready, 1)
            dve.wait_ge(bias_mm, 1)
            V.tensor_copy(wb[:, :], bank[4][:, 1:2]).then_inc(wb_ready, 1)
            link(V.tensor_scalar(bsc[:, 6:7], bank[4][:, 0:1], MIN_SQ, None, ALU.max))
            inverse_root(bsc[:, 2:3], bsc[:, 6:7], 1, link)
            V.tensor_tensor(bsc[:, 1:2], bsc[:, 6:7], bsc[:, 2:3], ALU.mult).then_inc(fn_asked, 1)

            def stats(n):
                dve.wait_ge(x_loaded[n], 16)
                for t in range(8 * n, 8 * n + 8):
                    ins = V.bn_stats(st6[:, t, :], xm[:, t, :])
                link(ins)
                for t in range(8 * n, 8 * n + 8):
                    ins = V.bn_aggr(mv[:, t, :], st6[:, t, :])
                link(ins)
                cols = slice(8 * n, 8 * n + 8)
                link(V.tensor_scalar(row[0][:, cols], mv[:, cols, 1], LN_EPS, None, ALU.add))
                inverse_root(row[1][:, cols], row[0][:, cols], 8, link)

            def normalize(n):
                for t in range(8 * n, 8 * n + 8):
                    ins = V.tensor_scalar(xm[:, t, :], xm[:, t, :], mv[:, t, 0:1], row[1][:, t:t + 1],
                                          ALU.subtract, ALU.mult)
                    if t % 4 == 3:
                        ins.then_inc(xn_ready, 1)

            def sum_squares(g):
                dve.wait_ge(mx_squared, g + 1)
                V.tensor_reduce(row[3][:, 4 * g:4 * g + 4], sq[:, g % 2, :].rearrange("p (t d) -> p t d", d=D),
                                AX_X, ALU.add).then_inc(sq_used, 1)

            stats(0)
            stats(1)
            normalize(0)
            stats(2)
            normalize(1)
            dve.wait_ge(fn_done, 1)
            link(V.scalar_tensor_tensor(out=bsc[:, 4:5], in0=bsc[:, 3:4], scalar=MAX_NORM, in1=bsc[:, 2:3],
                                        op0=ALU.min, op1=ALU.mult))
            fac = bsc[:, 4:5]
            link(V.tensor_tensor(bsc[:, 5:6], fac, fac, ALU.mult))
            link(V.tensor_tensor(bsc[:, 5:6], bsc[:, 5:6], bank[4][:, 0:1], ALU.mult))
            y2 = bsc[:, 5:6]
            sum_squares(0)
            stats(3)
            normalize(2)
            sum_squares(1)
            sum_squares(2)
            normalize(3)
            for g in range(3, QUADS):
                sum_squares(g)

            def stt(o, a, s, b, op0, op1):
                return V.scalar_tensor_tensor(out=o, in0=a, scalar=s, in1=b, op0=op0, op1=op1)

            def artanh(o, a, ask):
                link(V.tensor_scalar(row[10], a, CLIP, None, ALU.min))
                V.tensor_scalar(row[11], row[10], 0.25, None, ALU.is_ge).then_inc(fn_asked, 1)
                link(V.tensor_tensor(row[16], row[10], row[10], ALU.mult))
                link(V.tensor_scalar(row[17], row[16], ATANH_SERIES[0], None, ALU.mult))
                for c in ATANH_SERIES[1:]:
                    link(stt(row[17], row[17], c, row[16], ALU.add, ALU.mult))
                link(stt(row[17], row[17], 1.0, row[10], ALU.add, ALU.mult))
                dve.wait_ge(fn_done, ask)
                link(V.tensor_tensor(row[12], row[12], row[13], ALU.subtract))
                link(stt(row[12], row[12], 0.5, row[17], ALU.mult, ALU.subtract))
                link(V.tensor_tensor(row[12], row[12], row[11], ALU.mult))
                link(V.tensor_tensor(o, row[12], row[17], ALU.add))

            link(V.tensor_tensor(row[2], row[1], row[1], ALU.mult))
            link(stt(row[2], row[2], float(D), mv[:, :, 1], ALU.mult, ALU.mult))
            V.tensor_scalar(row[4], row[2], MIN_SQ, None, ALU.max)
            dve.wait_ge(sq_used, QUADS)
            link(V.tensor_scalar(row[5], row[3], MIN_SQ, None, ALU.max))
            def rows_of(first, count):
                return sc[:, first:first + count, :].rearrange("p a t -> p (a t)")

            inverse_root(rows_of(8, 2), rows_of(4, 2), 2 * KT, link)
            link(V.tensor_tensor(rows_of(6, 2), rows_of(4, 2), rows_of(8, 2), ALU.mult))
            dve.wait_ge(xb_in_psum, 1)
            link(V.tensor_scalar(row[18], bank[7][:, 0:KT], fac, None, ALU.mult))
            artanh(row[19], row[6], 3)
            link(V.tensor_tensor(row[14], row[7], row[8], ALU.mult))
            V.tensor_tensor(row[14], row[14], row[19], ALU.mult).then_inc(fn_asked, 1)
            dve.wait_ge(fn_done, 4)
            link(V.tensor_scalar(row[15], row[15], MAX_NORM, None, ALU.min))
            link(V.tensor_tensor(row[9], row[15], row[9], ALU.mult))
            link(V.tensor_tensor(row[15], row[15], row[15], ALU.mult))
            link(V.tensor_tensor(row[14], row[18], row[9], ALU.mult))
            link(V.tensor_scalar(row[14], row[14], 2.0, 1.0, ALU.mult, ALU.add))
            link(stt(row[16], row[15], y2, row[14], ALU.mult, ALU.add))
            link(V.tensor_scalar(row[16], row[16], MIN_NORM, None, ALU.max))
            link(V.reciprocal(row[16], row[16]))
            link(stt(row[14], row[14], y2, row[16], ALU.add, ALU.mult))
            link(V.tensor_tensor(row[20], row[14], row[9], ALU.mult))
            link(V.tensor_scalar(row[15], row[15], -1.0, 1.0, ALU.mult, ALU.add))
            link(V.tensor_tensor(row[21], row[15], row[16], ALU.mult))
            link(V.tensor_tensor(row[14], row[20], row[3], ALU.mult))
            link(stt(row[15], row[21], 2.0, row[18], ALU.mult, ALU.mult))
            link(V.tensor_tensor(row[14], row[14], row[15], ALU.add))
            link(V.tensor_tensor(row[14], row[14], row[20], ALU.mult))
            link(stt(row[15], row[21], y2, row[21], ALU.mult, ALU.mult))
            link(V.tensor_tensor(row[14], row[14], row[15], ALU.add))
            link(V.tensor_scalar(row[4], row[14], MIN_SQ, None, ALU.max))
            inverse_root(row[8], row[4], KT, link)
            link(V.tensor_tensor(row[6], row[4], row[8], ALU.mult))
            link(V.tensor_scalar(row[19], row[6], MAX_NORM, None, ALU.min))
            artanh(row[19], row[19], 6)
            link(V.tensor_tensor(row[19], row[19], row[8], ALU.mult))
            link(stt(row[21], row[21], fac, row[19], ALU.mult, ALU.mult))
            V.tensor_tensor(row[20], row[20], row[19], ALU.mult).then_inc(gains_ready, 1)

            def split_lo(b, c):
                for h in range(SUBS):
                    at = (c * SUBS + h) % PART
                    dve.wait_ge(hi_made, b * HALVES + c * SUBS + h + 1)
                    V.tensor_tensor(adj_lo[:, at, :], raw_c[c % RAW][:, h * SW:(h + 1) * SW],
                                    adj_hi[:, at, :].bitcast(F32), ALU.subtract).then_inc(lo_made, 1)

            def sum_quad(g):
                dve.wait_ge(mx_scaled, g + 1)
                for t in range(4 * g, 4 * g + 4):
                    ins = stt(xm[:, t, :], b_bc[:, :], row[21][:, t:t + 1], xm[:, t, :], ALU.mult, ALU.add)
                ins.then_inc(xt_sum, 1)

            def lo_quad(g):
                dve.wait_ge(xt_hi_made, g + 1)
                quad = slice(4 * g, 4 * g + 4)
                V.tensor_tensor(xt_lo[:, quad, :], xm[:, quad, :], xt_hi[:, quad, :].bitcast(F32),
                                ALU.subtract).then_inc(xt_ready, 1)

            LINKS = 1 + 11 + 1 + 7

            def post(b, par, step):
                g = [ga[:, k, :] for k in range(16)]
                per_tile = lambda ap: ap.rearrange("p (q d) -> p q d", d=D)

                linked = [(0, 12, 17)[step]]

                def chained(ins):
                    linked[0] += 1
                    ins.then_inc(ga_step, 1)
                    dve.wait_ge(ga_step, b * LINKS + linked[0])
                if step == 0:
                    dve.wait_ge(rows_squared, b + 1)
                    V.tensor_reduce(g[0], per_tile(sq[:, 0, :]), AX_X, ALU.add).then_inc(sums_read, 1)
                    dve.wait_ge(relu_squared, b + 1)
                    V.tensor_reduce(g[1], per_tile(sq[:, 1, :]), AX_X, ALU.add).then_inc(sums_read, 1)
                    dve.wait_ge(sums_read, 2 * b + 2)
                    pair = [ga[:, k:k + 2, :].rearrange("p a q -> p (a q)") for k in range(0, 8, 2)]
                    chained(V.tensor_scalar(pair[1], pair[0], MIN_SQ, None, ALU.max))
                    inverse_root(pair[2], pair[1], 2 * TILES, chained)
                if step == 1:
                    pair = [ga[:, k:k + 2, :].rearrange("p a q -> p (a q)") for k in range(0, 8, 2)]
                    chained(V.tensor_tensor(pair[3], pair[1], pair[2], ALU.mult))
                    chained(stt(g[8], g[6], ATANH_MAX, g[4], ALU.min, ALU.mult))
                    chained(V.tensor_tensor(g[9], g[7], g[8], ALU.mult))
                    chained(V.tensor_scalar(g[10], g[9], MIN_NORM, None, ALU.max))
                    V.reciprocal(g[12], g[10]).then_inc(tanh_asked, 1)
                    dve.wait_ge(tanh_asked, b + 1)
                    chained(V.tensor_tensor(g[13], g[8], g[12], ALU.mult))
                if step == 2:
                    dve.wait_ge(tanh_made, b + 1)
                    chained(stt(g[14], g[11], MAX_NORM, g[13], ALU.min, ALU.mult))
                    chained(V.tensor_copy(g[15], g[14]))
                    dve.wait_ge(xr_loaded[par], (b // 2 + 1) * 16 if isinstance(b, int) else (b - par) * 8 + 16)
                    for q in range(TILES):
                        V.scalar_tensor_tensor(out=xr[:, par, q, :], in0=rl[:, q * D:(q + 1) * D], scalar=ga[:, 15, q:q + 1],
                                               in1=xr[:, par, q, :], op0=ALU.mult, op1=ALU.add).then_inc(x2_ready, 1)
                    chained(V.tensor_copy(g[0], g[15]))

            def block_step(b, par):
                first = isinstance(b, int) and b == 0
                for c in range(CHUNKS):
                    if first:
                        sum_quad(c)
                        if c >= 1:
                            lo_quad(c - 1)
                        if c == CHUNKS - 1:
                            lo_quad(c)
                    split_lo(b, c)
                    if not first and c in DVE_POST_AT:
                        post(b - 1, 1 - par, DVE_POST_AT.index(c))
            blocks(dve, block_step)
            for step in range(3):
                post(BLOCKS - 1, 1, step)

            def relu_bias(s, par, lk, bank_n, dst, made, expert):
                for k in range(KH):
                    V.tensor_scalar(dst[:, k * P:(k + 1) * P], bank[bank_n][:, k * P:(k + 1) * P],
                                    bt[:, lk + k, bass.ds(expert, 1)], 0.0, ALU.add, ALU.max).then_inc(made, 1)

            def iteration(i, par):
                s, q = i - STATS, par
                if live(s):
                    dve.wait_ge(slot_loaded[q], (s - q) * 16 + 32)
                s, q = i - WO, par
                if live(s):
                    dve.wait_ge(wo_done, s + 1)
                    wait(dve, o_stored[q], (s - q) * 16)
                    V.tensor_tensor(f_o[q], bank[6][:, 0:D], bo_bc[:, :], ALU.add).then_inc(o_sum, 1)
                    dve.wait_ge(o_sum, s + 1)
                    V.tensor_tensor(f_o[q], f_o[q], raw[:, bass.ds(s * D, D)], ALU.add).then_inc(o_made, 1)
                s, q = i - T2, 1 - par
                if live(s):
                    e = dve.value_load(mint[0:1, 2, bass.ds(s, 1)], min_val=0, max_val=EXPERTS)
                    dve.wait_ge(t2_done, s + 1)
                    wait(dve, wo_done, s - 1)
                    relu_bias(s, q, KH, 5, f_h2[q], h2_made, e)
                s, q = i - T1, 1 - par
                if live(s):
                    e = dve.value_load(mint[0:1, 2, bass.ds(s, 1)], min_val=0, max_val=EXPERTS)
                    dve.wait_ge(t1_done, s + 1)
                    wait(dve, l1_done, s - 1)
                    relu_bias(s, q, 0, 3, f_h1[q], h1_made, e)
                s, q = i - STATS, par
                if live(s):
                    V.bn_stats(f_mv[:, q, 0:6], raw[:, bass.ds(s * D, D)]).then_inc(f_stats, 1)
                    dve.wait_ge(f_stats, s + 1)
                s, q = i - NORM, 1 - par
                if live(s):
                    dve.wait_ge(f_rstd, s + 1)
                    wait(dve, t0_done, s - 1)
                    V.tensor_scalar(f_xn[q], raw[:, bass.ds(s * D, D)], f_mv[:, q, 6:7], f_rs[:, q, :],
                                    ALU.subtract, ALU.mult).then_inc(f_xn_ready, 1)
                s, q = i - STATS, par
                if live(s):
                    V.bn_aggr(f_mv[:, q, 6:8], f_mv[:, q, 0:6]).then_inc(f_mean, 1)
                    dve.wait_ge(f_mean, s + 1)
                    V.tensor_scalar(f_mv[:, q, 8:9], f_mv[:, q, 7:8], LN_EPS, None, ALU.add).then_inc(f_var, 1)
            dve.wait_ge(weff_made, LAYERS * KH + 1)
            pipeline(dve, iteration)

        @block.tensor
        def _(pe):
            T = nc.tensor
            pe.wait_ge(consts_made, 3)
            pe.wait_ge(even_ready, 1)
            T.matmul(bank[5][0:GROUPS, 0:1], rt[4], rc[:, 2:3], start=True, stop=True).then_inc(slot_mm, 1)
            pe.wait_ge(lead_ready, 1)
            for k, (col, h) in enumerate(((rc[:, 7:8], 0), (ones[0:GROUPS, 0:1], 0), (r_f[:, GROUPS:GROUPS + 1], 0),
                                          (rc[:, 7:8], 1), (ones[0:GROUPS, 0:1], 1))):
                mm = T.matmul(bank[6][0:1, k * SLOTS:(k + 1) * SLOTS], col, lead[:, h, :], start=True, stop=True)
            mm.then_inc(tables_mm, 1)
            pe.wait_ge(wload, 16 * WLOADS)
            pe.wait_ge(bsq_ready, 1)
            T.matmul(bank[4][:, 0:1], ones[:, :], bsc[:, 0:1], start=True, stop=True)
            T.matmul(bank[4][:, 1:2], w_sb[:, :], b_col[:, :], start=True, stop=True).then_inc(bias_mm, 1)

            def transpose_quad(g):
                pe.wait_ge(xn_ready, g + 1)
                if g >= 2:
                    pe.wait_ge(xnt_copied, g - 1)
                for q in range(4):
                    mm = T.transpose(bank[g % 2][:, q * P:(q + 1) * P], xm[:, 4 * g + q, :], ident[:, :])
                mm.then_inc(xnt_in_psum, 1)

            transpose_quad(0)
            pe.wait_ge(wb_ready, 1)
            for g in range(QUADS):
                if g + 1 < QUADS:
                    transpose_quad(g + 1)
                pe.wait_ge(xnt_copied, g + 1)
                if g >= 2:
                    pe.wait_ge(mx_squared, g - 1)
                for q in range(4):
                    xnt = work[:, g % 2, q * P:(q + 1) * P]
                    mb = T.matmul(bank[7][:, 4 * g + q:4 * g + q + 1], xnt, wb[:, :], start=True, stop=True)
                    mm = T.matmul(bank[2 + g % 2][:, q * P:(q + 1) * P], xnt, wt_sb[:, :], start=True, stop=True)
                if g == QUADS - 1:
                    mb.then_inc(xb_in_psum, 1)
                mm.then_inc(mx_in_psum, 1)

            def rows_of_block(b, par):
                pe.wait_ge(support_copied, b + 1)
                wait(pe, relu_made, b - 1)
                for q in range(TILES):
                    mm = T.transpose(bank[2 + par][:, q * P:(q + 1) * P], work[:, par, q * P:(q + 1) * P], ident[:, :])
                mm.then_inc(rows_ready, 1)

            def block_step(b, par):
                first = isinstance(b, int) and b == 0
                wait(pe, support_copied, b - 1)
                for c in range(CHUNKS):
                    if first:
                        pe.wait_ge(xt_ready, c + 1)
                    for k in range(CK):
                        t = c * CK + k
                        half, k_in = c * SUBS + k // SK, k % SK
                        if k_in == 0:
                            pe.wait_ge(lo_made, b * HALVES + half + 1)
                        hi = adj_hi[:, half % PART, k_in * ROWS:(k_in + 1) * ROWS]
                        lo = adj_lo[:, half % PART, k_in * ROWS:(k_in + 1) * ROWS]
                        T.matmul(bank[par][:, :], xt_hi[:, t, :], hi, start=(t == 0), stop=False)
                        T.matmul(bank[par][:, :], xt_hi[:, t, :], lo, start=False, stop=False)
                        mm = T.matmul(bank[par][:, :], xt_lo[:, t, :], hi, start=False, stop=(t == KT - 1))
                        if k_in == SK - 1:
                            mm.then_inc(half_used, 1)
                    if c == CHUNKS - 1:
                        T.matmul(bank[5][:, 0:1], ident[:, :], ones[:, 0:1], start=True, stop=True).then_inc(support_ready, 1)
                    if not first and c == 2:
                        rows_of_block(b - 1, 1 - par)
            blocks(pe, block_step)
            rows_of_block(BLOCKS - 1, 1)

            def routed(s, q, lk, h, bank_n, done):
                e = pe.value_load(mint[0:1, 2, bass.ds(s, 1)], min_val=0, max_val=EXPERTS)
                for k in range(KH):
                    mm = T.matmul(bank[bank_n][:, 0:HID], h[q][:, k * P:(k + 1) * P],
                                  weff[:, lk + k, bass.ds(e, 1), :].rearrange("p a n -> p (a n)"),
                                  start=(k == 0), stop=(k == KH - 1))
                mm.then_inc(done, 1)

            def back(s, q, u, bank_n, done):
                for k in range(KH):
                    mm = T.transpose(bank[bank_n][:, k * P:(k + 1) * P], u[q][:, k * P:(k + 1) * P], ident[:, :])
                mm.then_inc(done, 1)

            def iteration(i, par):
                s, q = i - WO, par
                if live(s):
                    pe.wait_ge(h2_made, KH * s + KH)
                    wait(pe, o_sum, s)
                    for k in range(KH):
                        mm = T.matmul(bank[6][:, 0:D], f_h2[q][:, k * P:(k + 1) * P], wo_sb[:, k, :],
                                      start=(k == 0), stop=(k == KH - 1))
                    mm.then_inc(wo_done, 1)
                s, q = i - T2, 1 - par
                if live(s):
                    pe.wait_ge(u1_made, s + 1)
                    wait(pe, h2_made, KH * s)
                    back(s, q, f_u1, 5, t2_done)
                s, q = i - L1, par
                if live(s):
                    pe.wait_ge(h1_made, KH * s + KH)
                    wait(pe, u1_made, s)
                    routed(s, q, KH, f_h1, 4, l1_done)
                s, q = i - T1, 1 - par
                if live(s):
                    pe.wait_ge(u0_made, s + 1)
                    wait(pe, h1_made, KH * s)
                    back(s, q, f_u0, 3, t1_done)
                s, q = i - L0, par
                if live(s):
                    pe.wait_ge(h0_made, KH * s + KH)
                    wait(pe, u0_made, s)
                    routed(s, q, 0, f_h0, 2, l0_done)
                s, q = i - WI, 1 - par
                if live(s):
                    pe.wait_ge(xt_copied, s + 1)
                    wait(pe, h0_made, KH * s)
                    for k in range(KH):
                        mm = T.matmul(bank[1][:, k * P:(k + 1) * P], wi_sb[:, k * P:(k + 1) * P], f_xt[q],
                                      start=True, stop=True)
                    mm.then_inc(wi_done, 1)
                s, q = i - T0, par
                if live(s):
                    pe.wait_ge(f_xn_ready, s + 1)
                    wait(pe, xt_copied, s)
                    T.transpose(bank[0][:, 0:P], f_xn[q], ident[:, :]).then_inc(t0_done, 1)
            pe.wait_ge(meta_ready, 1)
            pe.wait_ge(weff_made, LAYERS * KH + 1)
            pe.wait_ge(relu_made, BLOCKS)
            pipeline(pe, iteration)


def kernel(**inputs):
    import concourse.bacc as bacc
    from concourse.bass_utils import run_bass_kernel_spmd as run

    nc = bacc.Bacc("TRN2", target_bir_lowering=False, num_devices=1)
    arrays = {}

    def dram(name, a):
        a = np.ascontiguousarray(a)
        arrays[name] = a
        return nc.dram_tensor(name, a.shape, mybir.dt.from_np(a.dtype), kind="ExternalInput").ap()

    def get(name):
        return np.asarray(inputs[name])

    def by_partition(a):
        n = a.shape[1]
        a = a.transpose(0, 3, 1, 2).reshape(LAYERS, KH, P, n, HID)
        return a.transpose(2, 0, 1, 3, 4).reshape(P, LAYERS * KH, n, HID)

    def bias_by_partition(a):
        n = a.shape[1]
        return a.reshape(LAYERS, n, KH, P).transpose(3, 0, 2, 1).reshape(P, LAYERS * KH, n)

    w = get("L0_gnn_weight")
    args = [
        dram("x", get("x")),
        dram("adj_t", get("adj").reshape(BLOCKS, ROWS, P, KT).transpose(0, 2, 3, 1).reshape(BLOCKS, P, KT * ROWS)),
        dram("w", w),
        dram("w_t", w.T),
        dram("bias", get("L0_gnn_bias")),
        dram("route", get("L0_ffn_route_id")),
        dram("wi_t", get("L0_ffn_Wi").T),
        dram("bi", get("L0_ffn_bi").reshape(KH, P).T),
        dram("wr_t", by_partition(get("L0_ffn_Wr"))),
        dram("ws_t", by_partition(get("L0_ffn_Ws"))[:, :, 0, :]),
        dram("b_t", np.concatenate([bias_by_partition(get("L0_ffn_br")), bias_by_partition(get("L0_ffn_bs"))], axis=2)),
        dram("wo_t", get("L0_ffn_Wo").T.reshape(KH, P, D).transpose(1, 0, 2)),
        dram("bo", get("L0_ffn_bo")),
        nc.dram_tensor("x2_dram", (N, D), F32, kind="Internal").ap(),
        nc.dram_tensor("out", ((GROUPS + 2 * SLOTS) * GR, D), F32, kind="ExternalOutput").ap(),
    ]
    build(nc, *args)
    r = run(nc, [arrays], core_ids=[0])
    return r.results[0]["out"][:N]
```

```python
from contextlib import ExitStack

import numpy as np

import concourse.bass as bass
from concourse import mybir

F32 = mybir.dt.float32
F32R = mybir.dt.float32r
I32 = mybir.dt.int32
ALU = mybir.AluOpType
ACT = mybir.ActivationFunctionType
AX_X = mybir.AxisListType.X

P = 128
N = 4096
D = 128
HID = 256
KT = N // P
ROWS = 512
BLOCKS = N // ROWS
TILES = ROWS // P
CK = 4
CHUNKS = KT // CK
CW = CK * ROWS
RAW = 4
SUBS = 2
PART = 4
SW = CW // SUBS
SK = CK // SUBS
HALVES = CHUNKS * SUBS

LAYERS, EXPERTS = 2, 16
E1 = EXPERTS + 1
GROUPS = 64
GR = N // GROUPS
SLOTS = (GROUPS + E1) // 2
KH = HID // P
HB = HID + 1

MIN_NORM = 1e-15
MIN_SQ = 1e-30
MAX_NORM = float(np.float32(1.0 - 1e-5))
CLIP = float(np.float32(1.0 - 1e-7))
ATANH_MAX = float(np.arctanh(np.float64(np.float32(1.0 - 1e-5))))
LN_EPS = 1e-5
ATANH_SERIES = [1.0 / 13, 1.0 / 11, 1.0 / 9, 1.0 / 7, 1.0 / 5, 1.0 / 3]

GATHER, COPY, WI, L0, L1, WO = -1, (-1, 0), 0, 1, 2, 3
HEAD = range(GATHER, 4)
BODY = (4, SLOTS - 2)
TAIL = range(SLOTS - 2, SLOTS + WO)
POST_AT = [1, 4, 6]
DVE_POST_AT = [4, 5, 6, 7]
FINAL_AT = 2


def build(nc, x, adj_t, w, w_t, bias, route, wi_t, bi, wr_t, ws_t, wo_t, bo, x2t_dram, out_t):
    with ExitStack() as ctx:
        def sb(name, shape, dt=F32):
            return ctx.enter_context(nc.sbuf_tensor(name, shape, dt))

        def sem(name):
            return ctx.enter_context(nc.semaphore(name))

        bank = [ctx.enter_context(nc.psum_tensor(f"bank{i}", [P, 512], F32)) for i in range(8)]

        xm = sb("xm", [P, KT, D])
        xt_hi = sb("xt_hi", [P, KT, D], F32R)
        xt_lo = sb("xt_lo", [P, KT, D], F32R)
        raw = sb("raw", [P, RAW * CW])
        adj_hi = sb("adj_hi", [P, PART, SW], F32R)
        adj_lo = sb("adj_lo", [P, PART, SW], F32R)
        weff = sb("weff", [P, LAYERS * KH, E1, HB])
        wi_sb = sb("wi_sb", [P, HID])
        bi_sb = sb("bi_sb", [P, KH])
        wo_sb = sb("wo_sb", [P, KH, D])
        bo_col = sb("bo_col", [P, 1])
        b_col = sb("b_col", [P, 1])
        b_bc = sb("b_bc", [P, D])
        ident = sb("ident", [P, P])
        ones = sb("ones", [P, P])
        work = sb("work", [P, 2, 512])
        sq = sb("sq", [P, 2, 512])
        rl = sb("rl", [P, 512])
        xr = sb("xr", [P, 2, TILES, D])
        st6 = sb("st6", [P, KT, 6])
        mv = sb("mv", [P, KT, 2])
        wb = sb("wb", [P, 1])
        sc = sb("sc", [P, 22, KT])
        row = [sc[:, n, :] for n in range(22)]
        bsc = sb("bsc", [P, 8])
        tmp_i = sb("tmp_i", [P, 2 * KT], I32)
        tmp_f = sb("tmp_f", [P, 2 * KT])
        f_expo = sb("f_expo", [P, 1])
        ga = sb("ga", [P, 16, TILES])
        x2t_out = sb("x2t_out", [P, ROWS])
        w_sb, wt_sb = x2t_out[:, 0:D], x2t_out[:, D:2 * D]
        st6_b = sb("st6_b", [P, TILES, 6])
        mv_b = sb("mv_b", [P, TILES, 2])
        var_b = sb("var_b", [P, TILES, 1])
        rstd_b = sb("rstd_b", [P, TILES, 1])
        r_int = sb("r_int", [GROUPS, GROUPS + 1], I32)
        r_f = sb("r_f", [GROUPS, GROUPS + 1])
        valid = sb("valid", [GROUPS, GROUPS + 1])
        later = rl[0:GROUPS, 0:GROUPS]
        earlier = rl[0:GROUPS, GROUPS:2 * GROUPS]
        rt = [rl[0:GROUPS, (2 + n) * GROUPS:(3 + n) * GROUPS] for n in range(5)]
        rc = sb("rc", [GROUPS, 8])
        rci = sb("rci", [GROUPS, 2], I32)
        iota_f = x2t_out[0:GROUPS, 2 * D:2 * D + SLOTS]
        lead = x2t_out[0:GROUPS, 2 * D + SLOTS:2 * D + 3 * SLOTS].rearrange("p (a s) -> p a s", a=2)
        mrow = sb("mrow", [1, 8, SLOTS])
        trash = sb("trash", [1, SLOTS // 2, 2])
        mint = sb("mint", [1, 5, SLOTS], I32)
        xnt = xm[:, :, :].rearrange("p t d -> p (t d)")
        TRASH = GROUPS
        RINGS = (GROUPS + 4) * GR

        def ring(at, width):
            return [raw[:, RINGS + at + n * width:RINGS + at + (n + 1) * width] for n in range(2)]

        f_xt = [work[:, n, 0:P] for n in range(2)]
        f_w = [ring(6 * HID + layer * 2 * KH * HB, KH * HB) for layer in range(LAYERS)]
        f_h0, f_h1, f_h2 = (ring(n * 2 * HID, HID) for n in range(3))

        x_loaded = [sem(f"x_loaded{n}") for n in range(4)]
        wload = sem("wload")
        route_loaded = sem("route_loaded")
        wr_loaded = sem("wr_loaded")
        pool_step = sem("pool_step")
        consts_made = sem("consts_made")
        dve_step = sem("dve_step")
        act_step = sem("act_step")
        even_ready = sem("even_ready")
        slot_mm = sem("slot_mm")
        lead_ready = sem("lead_ready")
        tables_mm = sem("tables_mm")
        meta_ready = sem("meta_ready")
        bsq_ready = sem("bsq_ready")
        bias_mm = sem("bias_mm")
        wb_ready = sem("wb_ready")
        xn_ready = sem("xn_ready")
        xnt_in_psum = sem("xnt_in_psum")
        xnt_copied = sem("xnt_copied")
        mx_in_psum = sem("mx_in_psum")
        xb_in_psum = sem("xb_in_psum")
        mx_copied = sem("mx_copied")
        mx_squared = sem("mx_squared")
        sq_used = sem("sq_used")
        fn_asked = sem("fn_asked")
        fn_done = sem("fn_done")
        gains_ready = sem("gains_ready")
        mx_scaled = sem("mx_scaled")
        xt_sum = sem("xt_sum")
        xt_hi_made = sem("xt_hi_made")
        xt_ready = sem("xt_ready")
        adj_loaded = [sem(f"adj_loaded{n}") for n in range(RAW)]
        hi_made = sem("hi_made")
        lo_made = sem("lo_made")
        half_used = sem("half_used")
        support_ready = sem("support_ready")
        support_copied = sem("support_copied")
        rows_ready = sem("rows_ready")
        rows_squared = sem("rows_squared")
        relu_made = sem("relu_made")
        relu_squared = sem("relu_squared")
        sums_read = sem("sums_read")
        tanh_asked = sem("tanh_asked")
        tanh_made = sem("tanh_made")
        ga_step = sem("ga_step")
        xr_loaded = [sem(f"xr_loaded{n}") for n in range(2)]
        x2_ready = sem("x2_ready")
        norms_asked = sem("norms_asked")
        norms_rooted = sem("norms_rooted")
        stats_b = sem("stats_b")
        mean_b = sem("mean_b")
        var_ready = sem("var_ready")
        rstd_ready = sem("rstd_ready")
        centred = sem("centred")
        ln_ready = sem("ln_ready")
        turned = sem("turned")
        turned_copied = sem("turned_copied")
        x2t_stored = sem("x2t_stored")
        x2t_loaded = sem("x2t_loaded")
        weff_made = sem("weff_made")
        trash_made = sem("trash_made")
        gathered = sem("gathered")
        wi_done = sem("wi_done")
        h0_made = sem("h0_made")
        w_copied = [sem(f"w_copied{layer}") for layer in range(LAYERS)]
        l0_done = sem("l0_done")
        h1_made = sem("h1_made")
        l1_done = sem("l1_done")
        h2_made = sem("h2_made")
        wo_done = sem("wo_done")
        o_made = sem("o_made")
        o_stored = sem("o_stored")

        def wait(eng, semaphore, value):
            if isinstance(value, int) and value <= 0:
                return
            eng.wait_ge(semaphore, value)

        def blocks(eng, block_step):
            block_step(0, 0)
            block_step(1, 1)
            with eng.Fori(1, BLOCKS // 2) as pair:
                block_step(pair * 2, 0)
                block_step(pair * 2 + 1, 1)

        def pipeline(eng, iteration):
            for i in HEAD:
                iteration(i, i % 2)
            with eng.Fori(BODY[0] // 2, BODY[1] // 2) as pair:
                iteration(pair * 2, 0)
                iteration(pair * 2 + 1, 1)
            for i in TAIL:
                iteration(i, i % 2)

        def live(slot):
            return not isinstance(slot, int) or 0 <= slot < SLOTS

        raw_c = [raw[:, r * CW:(r + 1) * CW] for r in range(RAW)]
        WLOADS = 9
        QUADS = KT // 4

        block = ctx.enter_context(nc.Block())

        @block.sync
        def _(sp):
            sp.dma_start(r_int[:, 0:GROUPS], route.rearrange("(a n) -> a n", a=1).to_broadcast([GROUPS, GROUPS])).then_inc(route_loaded, 16)
            sp.dma_start(r_int[:, GROUPS:GROUPS + 1], route.rearrange("(n a) -> n a", a=1)).then_inc(route_loaded, 16)
            for n in range(4):
                sp.dma_start(xm[:, n * 8:(n + 1) * 8, :],
                             x.rearrange("(p t) d -> p t d", p=P)[:, n * 8:(n + 1) * 8, :]).then_inc(x_loaded[n], 16)
            sp.dma_start(w_sb, w).then_inc(wload, 16)
            sp.dma_start(wt_sb, w_t).then_inc(wload, 16)
            sp.dma_start(b_col[:, :], bias.rearrange("(p a) -> p a", a=1)).then_inc(wload, 16)
            sp.dma_start(b_bc[:, :], bias.rearrange("(a n) -> a n", a=1).to_broadcast([P, D])).then_inc(wload, 16)
            sp.dma_start(wi_sb[:, :], wi_t).then_inc(wload, 16)
            sp.dma_start(bi_sb[:, :], bi).then_inc(wload, 16)
            sp.dma_start(wo_sb[:, :, :], wo_t).then_inc(wload, 16)
            sp.dma_start(bo_col[:, :], bo.rearrange("(p a) -> p a", a=1)).then_inc(wload, 16)
            sp.dma_start(weff[:, :, EXPERTS, :], ws_t).then_inc(wload, 16)
            for c in range(RAW):
                sp.dma_start(raw_c[c], adj_t[0, :, c * CW:(c + 1) * CW]).then_inc(adj_loaded[c], 16)
            for lk in range(LAYERS * KH):
                sp.dma_start(weff[:, lk, 0:EXPERTS, :], wr_t[:, lk, :, :]).then_inc(wr_loaded, 16)

            def load_block(b, par):
                for c in range(CHUNKS):
                    if isinstance(b, int) and b * CHUNKS + c < RAW:
                        continue
                    sp.wait_ge(lo_made, (b * CHUNKS + c - RAW + 1) * SUBS)
                    sp.dma_start(raw_c[c % RAW], adj_t[bass.ds(b, 1), :, c * CW:(c + 1) * CW].rearrange("a p n -> (a p) n")
                                 ).then_inc(adj_loaded[c % RAW], 16)
            blocks(sp, load_block)

            sp.wait_ge(x2t_stored, (BLOCKS - 1) * 16)
            sp.wait_ge(lo_made, BLOCKS * HALVES)
            kept = N - ROWS
            sp.dma_start(raw[:, 0:kept], x2t_dram[:, 0:kept]).then_inc(x2t_loaded, 16)

            sp.wait_ge(o_made, 2 * SLOTS)
            for n in range(4):
                cols = slice(n * N // 4, (n + 1) * N // 4)
                sp.dma_start(out_t[:, cols], raw[:, cols]).then_inc(o_stored, 16)
            sp.wait_ge(o_stored, 4 * 16)

        @block.gpsimd
        def _(pool):
            steps = 0
            for dst, val in ((ident[:, :], 0.0), (ones[:, :], 1.0), (later, 1.0), (earlier, 1.0),
                             (f_expo[:, :], -0.5)):
                nc.gpsimd.memset(dst, val).then_inc(pool_step, 1)
                steps += 1
            nc.gpsimd.iota(iota_f[:, :], pattern=[[1, SLOTS]], base=0, channel_multiplier=0,
                           allow_small_or_imprecise_dtypes=True).then_inc(pool_step, 1)
            nc.gpsimd.iota(rc[:, 7:8], pattern=[[0, 1]], base=0, channel_multiplier=1,
                           allow_small_or_imprecise_dtypes=True).then_inc(pool_step, 1)
            steps += 2
            pool.wait_ge(pool_step, steps)
            nc.gpsimd.affine_select(out=ident[:, :], in_=ident[:, :], compare_op=ALU.not_equal, fill=1.0, base=0,
                                    pattern=[[-1, P]], channel_multiplier=1).then_inc(consts_made, 1)
            nc.gpsimd.affine_select(out=later, in_=later, compare_op=ALU.is_gt, fill=0.0, base=0,
                                    pattern=[[1, GROUPS]], channel_multiplier=-1).then_inc(consts_made, 1)
            nc.gpsimd.affine_select(out=earlier, in_=earlier, compare_op=ALU.is_gt, fill=0.0, base=0,
                                    pattern=[[-1, GROUPS]], channel_multiplier=1).then_inc(consts_made, 1)

            pool.wait_ge(consts_made, 3)
            pool.wait_ge(wload, 16 * WLOADS)
            pool.wait_ge(wr_loaded, 16 * LAYERS * KH)
            for lk in range(LAYERS * KH):
                diag = weff[:, lk, EXPERTS, (lk % KH) * P:(lk % KH + 1) * P]
                nc.gpsimd.tensor_tensor(diag, diag, ident[:, :], ALU.add).then_inc(pool_step, 1)
                pool.wait_ge(pool_step, steps + lk + 1)
                nc.gpsimd.tensor_tensor(weff[:, lk, 0:EXPERTS, :], weff[:, lk, 0:EXPERTS, :],
                                        weff[:, lk, EXPERTS:E1, :].to_broadcast([P, EXPERTS, HB]), ALU.add).then_inc(weff_made, 1)
            pool.dma_start(xr[:, 0, :, :], x[0:ROWS, :].rearrange("(q p) d -> p q d", p=P)).then_inc(xr_loaded[0], 16)

            expo = f_expo[:, :].to_broadcast([P, 2 * TILES])
            expo_b = f_expo[:, :].rearrange("p (a n) -> p a n", a=1).to_broadcast([P, TILES, 1])

            def block_step(b, par, last=False):
                if not last:
                    wait(pool, turned, b)
                    pool.dma_start(xr[:, 1 - par, :, :], x[bass.ds(b * ROWS + ROWS, ROWS), :].rearrange("(q p) d -> p q d", p=P)
                                   ).then_inc(xr_loaded[1 - par], 16)
                pool.wait_ge(norms_asked, b + 1)
                nc.gpsimd.tensor_tensor(ga[:, 4:6, :].rearrange("p a q -> p (a q)"), ga[:, 2:4, :].rearrange("p a q -> p (a q)"),
                                        expo, ALU.pow).then_inc(norms_rooted, 1)
                pool.wait_ge(var_ready, b + 1)
                nc.gpsimd.tensor_tensor(rstd_b[:, :, :], var_b[:, :, :], expo_b, ALU.pow).then_inc(rstd_ready, 1)
                rows = rl[:, :].rearrange("p (q d) -> p q d", d=D)
                nc.gpsimd.tensor_tensor(rows, xr[:, par, :, :], mv_b[:, :, 0:1].to_broadcast([P, TILES, D]),
                                        ALU.subtract).then_inc(centred, 1)
                pool.wait_ge(rstd_ready, b + 1)
                pool.wait_ge(centred, b + 1)
                nc.gpsimd.tensor_tensor(rows, rows, rstd_b[:, :, :].to_broadcast([P, TILES, D]), ALU.mult).then_inc(ln_ready, 1)
                if not last:
                    pool.wait_ge(turned_copied, 2 * b + 2)
                    pool.dma_start(x2t_dram[:, bass.ds(b * ROWS, ROWS)], x2t_out[:, :]).then_inc(x2t_stored, 16)

            block_step(0, 0)
            block_step(1, 1)
            with pool.Fori(1, BLOCKS // 2 - 1) as pair:
                block_step(pair * 2, 0)
                block_step(pair * 2 + 1, 1)
            block_step(BLOCKS - 2, 0)
            block_step(BLOCKS - 1, 1, last=True)

            pool.wait_ge(lo_made, BLOCKS * HALVES)
            nc.gpsimd.memset(raw[:, TRASH * GR:(TRASH + 4) * GR], 0.0).then_inc(trash_made, 1)
            pool.wait_ge(turned_copied, 2 * BLOCKS)
            pool.wait_ge(meta_ready, 1)

            def iteration(i, par):
                s, q = i - GATHER, 1 - par
                if live(s):
                    wait(pool, wi_done, s - 1)
                    for g in range(2):
                        src = pool.value_load(mint[0:1, g, bass.ds(s, 1)], min_val=0, max_val=GROUPS - 1)
                        nc.gpsimd.tensor_copy(f_xt[q][:, g * GR:(g + 1) * GR], xnt[:, bass.ds(src * GR, GR)]).then_inc(gathered, 1)
            pipeline(pool, iteration)

        @block.scalar
        def _(act):
            act.wait_ge(fn_asked, 1)
            nc.scalar.activation(bsc[:, 3:4], bsc[:, 1:2], ACT.Tanh).then_inc(fn_done, 1)

            def copy_xnt(g):
                act.wait_ge(xnt_in_psum, g + 1)
                if g >= 2:
                    act.wait_ge(mx_in_psum, g - 1)
                nc.scalar.activation(work[:, g % 2, :], bank[g % 2][:, :], ACT.Copy).then_inc(xnt_copied, 1)

            copy_xnt(0)
            for g in range(QUADS):
                if g + 1 < QUADS:
                    copy_xnt(g + 1)
                act.wait_ge(mx_in_psum, g + 1)
                mx = bank[2 + g % 2][:, :]
                nc.scalar.activation(xm[:, 4 * g:4 * g + 4, :].rearrange("p t d -> p (t d)"), mx, ACT.Copy).then_inc(mx_copied, 1)
                if g >= 2:
                    act.wait_ge(sq_used, g - 1)
                nc.scalar.activation(sq[:, g % 2, :], mx, ACT.Square).then_inc(mx_squared, 1)

            def logs(asked):
                act.wait_ge(fn_asked, asked)
                nc.scalar.activation(row[12], row[10], ACT.Ln, bias=1.0).then_inc(fn_done, 1)
                nc.scalar.activation(row[13], row[10], ACT.Ln, bias=1.0, scale=-1.0).then_inc(fn_done, 1)

            logs(2)
            act.wait_ge(fn_asked, 3)
            nc.scalar.activation(row[15], row[14], ACT.Tanh).then_inc(fn_done, 1)
            logs(4)
            act.wait_ge(gains_ready, 1)
            def split_hi(b, c):
                act.wait_ge(adj_loaded[c % RAW], b * (CHUNKS // RAW * 16) + (c // RAW + 1) * 16)
                for h in range(SUBS):
                    wait(act, half_used, b * HALVES + c * SUBS + h - PART + 1)
                    nc.scalar.activation(adj_hi[:, (c * SUBS + h) % PART, :], raw_c[c % RAW][:, h * SW:(h + 1) * SW],
                                         ACT.Copy).then_inc(hi_made, 1)

            def scale_quad(g):
                for t in range(4 * g, 4 * g + 4):
                    mm = nc.scalar.activation(xm[:, t, :], xm[:, t, :], ACT.Copy, scale=row[20][:, t:t + 1])
                mm.then_inc(mx_scaled, 1)

            def hi_quad(g):
                act.wait_ge(xt_sum, g + 1)
                nc.scalar.activation(xt_hi[:, 4 * g:4 * g + 4, :], xm[:, 4 * g:4 * g + 4, :], ACT.Copy).then_inc(xt_hi_made, 1)

            def post(b, par, step):
                rows = bank[2 + par][:, :]
                if step == 0:
                    act.wait_ge(support_ready, b + 1)
                    nc.scalar.activation(work[:, par, :], bank[par][:, :], ACT.Copy).then_inc(support_copied, 1)
                if step == 1:
                    act.wait_ge(rows_ready, b + 1)
                    wait(act, sums_read, 2 * b)
                    nc.scalar.activation(sq[:, 0, :], rows, ACT.Square).then_inc(rows_squared, 1)
                    wait(act, x2_ready, b * TILES)
                    nc.scalar.activation(rl[:, :], rows, ACT.Relu).then_inc(relu_made, 1)
                    act.wait_ge(relu_made, b + 1)
                    nc.scalar.activation(sq[:, 1, :], rl[:, :], ACT.Square).then_inc(relu_squared, 1)
                if step == 2:
                    act.wait_ge(tanh_asked, b + 1)
                    nc.scalar.activation(ga[:, 11, :], ga[:, 10, :], ACT.Tanh).then_inc(tanh_made, 1)

            def final(b, x2t):
                act.wait_ge(turned, b + 1)
                wait(act, x2t_stored, b * 16)
                nc.scalar.activation(x2t, bank[6][:, :], ACT.Copy).then_inc(turned_copied, 1)
                nc.scalar.activation(xnt[:, bass.ds(b * ROWS, ROWS)], bank[4][:, :], ACT.Copy).then_inc(turned_copied, 1)

            def block_step(b, par):
                first = isinstance(b, int) and b == 0
                for c in range(CHUNKS):
                    if first:
                        scale_quad(c)
                        if c >= 1:
                            hi_quad(c - 1)
                        if c == CHUNKS - 1:
                            hi_quad(c)
                    split_hi(b, c)
                    if not first and c in POST_AT:
                        post(b - 1, 1 - par, POST_AT.index(c))
                    if c == FINAL_AT and not (isinstance(b, int) and b < 2):
                        final(b - 2, x2t_out[:, :])
            blocks(act, block_step)
            post(BLOCKS - 1, 1, 0)
            final(BLOCKS - 2, x2t_out[:, :])
            post(BLOCKS - 1, 1, 1)
            post(BLOCKS - 1, 1, 2)
            act.wait_ge(lo_made, BLOCKS * HALVES)
            final(BLOCKS - 1, raw[:, N - ROWS:N])

            def ready_to_copy(i):
                if live(i - 1):
                    act.wait_ge(h1_made, KH * i)
                elif live(i - 2):
                    act.wait_ge(h2_made, KH * i - KH)

            def iteration(i, par):
                s, q = i - WI, par
                if live(s):
                    act.wait_ge(wi_done, s + 1)
                    for k in range(KH):
                        if k == KH - 1:
                            ready_to_copy(i)
                        nc.scalar.activation(f_h0[q][:, k * P:(k + 1) * P], bank[4 * q][:, k * P:(k + 1) * P], ACT.Relu,
                                             bias=bi_sb[:, k:k + 1]).then_inc(h0_made, 1)
                else:
                    ready_to_copy(i)
                for layer in range(LAYERS):
                    s = i - COPY[layer]
                    q = (par - COPY[layer]) % 2
                    if live(s):
                        e = act.value_load(mint[0:1, 2, bass.ds(s, 1)], min_val=0, max_val=EXPERTS)
                        nc.scalar.activation(f_w[layer][q].rearrange("p (k n) -> p k n", n=HB),
                                             weff[:, layer * KH:(layer + 1) * KH, bass.ds(e, 1), :].rearrange("p k a n -> p k (a n)"),
                                             ACT.Copy).then_inc(w_copied[layer], 1)
            act.wait_ge(half_used, BLOCKS * HALVES)
            act.wait_ge(weff_made, LAYERS * KH)
            pipeline(act, iteration)

        @block.vector
        def _(dve):
            chain = [0]

            def link(ins):
                chain[0] += 1
                ins.then_inc(dve_step, 1)
                dve.wait_ge(dve_step, chain[0])

            V = nc.vector
            dve.wait_ge(route_loaded, 32)
            link(V.tensor_copy(r_f[:, :], r_int[:, :]))
            link(V.tensor_scalar(valid[:, :], r_f[:, :], 0.0, None, ALU.is_ge))
            link(V.scalar_tensor_tensor(out=valid[:, :], in0=r_f[:, :], scalar=float(EXPERTS - 1), in1=valid[:, :],
                                        op0=ALU.is_le, op1=ALU.mult))
            link(V.scalar_tensor_tensor(out=r_f[:, :], in0=r_f[:, :], scalar=-float(EXPERTS), in1=valid[:, :],
                                        op0=ALU.add, op1=ALU.mult))
            link(V.tensor_scalar(r_f[:, :], r_f[:, :], float(EXPERTS), None, ALU.add))
            own = r_f[:, GROUPS:GROUPS + 1]
            dve.wait_ge(consts_made, 3)
            V.tensor_scalar(rt[1], r_f[:, 0:GROUPS], own, None, ALU.is_gt)
            link(V.tensor_scalar(rt[0], r_f[:, 0:GROUPS], own, None, ALU.is_equal))
            V.tensor_tensor(rt[2], rt[0], later, ALU.mult)
            link(V.tensor_tensor(rt[3], rt[0], earlier, ALU.mult))
            link(V.tensor_reduce(rc[:, 0:1], rt[3], AX_X, ALU.add))
            link(V.tensor_copy(rci[:, 0:1], rc[:, 0:1]))
            link(V.tensor_scalar(rci[:, 1:2], rci[:, 0:1], 1, None, ALU.bitwise_and))
            link(V.tensor_copy(rc[:, 1:2], rci[:, 1:2]))
            link(V.tensor_scalar(rc[:, 2:3], rc[:, 1:2], -1.0, 1.0, ALU.mult, ALU.add))
            V.tensor_tensor(rt[4], rt[1], rt[2], ALU.add).then_inc(even_ready, 1)
            dve.wait_ge(slot_mm, 1)
            link(V.tensor_tensor(rc[:, 3:4], bank[5][0:GROUPS, 0:1], rc[:, 1:2], ALU.subtract))
            V.tensor_scalar(lead[:, 0, :], iota_f[:, :], rc[:, 3:4], rc[:, 2:3], ALU.is_equal, ALU.mult)
            V.tensor_scalar(lead[:, 1, :], iota_f[:, :], rc[:, 3:4], rc[:, 1:2], ALU.is_equal, ALU.mult).then_inc(lead_ready, 1)
            dve.wait_ge(tables_mm, 1)
            link(V.tensor_copy(mrow[0:1, 0:5, :].rearrange("a k s -> a (k s)"), bank[6][0:1, 0:5 * SLOTS]))
            m = [mrow[0:1, k, :] for k in range(8)]
            link(V.tensor_scalar(m[4], m[4], -1.0, 1.0, ALU.mult, ALU.add))
            link(V.tensor_tensor(m[5], m[4], m[0], ALU.mult))
            link(V.tensor_tensor(m[5], m[5], m[3], ALU.add))
            link(V.tensor_scalar(m[1], m[1], -1.0, 1.0, ALU.mult, ALU.add))
            V.memset(trash[:, :, 0], float(TRASH))
            link(V.memset(trash[:, :, 1], float(TRASH + 2)))
            flat_trash = trash[:, :, :].rearrange("a s two -> a (s two)")
            V.tensor_tensor(m[6], m[1], flat_trash, ALU.mult)
            link(V.scalar_tensor_tensor(out=m[7], in0=flat_trash, scalar=1.0, in1=m[4], op0=ALU.add, op1=ALU.mult))
            V.tensor_tensor(m[6], m[6], m[0], ALU.add)
            link(V.tensor_tensor(m[7], m[7], m[3], ALU.add))
            for k, src in enumerate((0, 5, 2, 6, 7)):
                ins = V.tensor_copy(mint[0:1, k, :], m[src])
            ins.then_inc(meta_ready, 1)

            def inverse_root(dst, src, width, chained):
                ti, tf = tmp_i[:, 0:width], tmp_f[:, 0:width]
                chained(V.tensor_scalar(ti, src.bitcast(I32), 1, None, ALU.logical_shift_right))
                chained(V.tensor_scalar(dst.bitcast(I32), ti, -1.0, float(0x5F3759DF), ALU.mult, ALU.add))
                for _ in range(3):
                    chained(V.tensor_tensor(tf, dst, dst, ALU.mult))
                    chained(V.scalar_tensor_tensor(out=tf, in0=tf, scalar=-0.5, in1=src, op0=ALU.mult, op1=ALU.mult))
                    chained(V.scalar_tensor_tensor(out=dst, in0=tf, scalar=1.5, in1=dst, op0=ALU.add, op1=ALU.mult))

            dve.wait_ge(wload, 16 * WLOADS)
            V.tensor_tensor(bsc[:, 0:1], b_col[:, :], b_col[:, :], ALU.mult).then_inc(bsq_ready, 1)
            dve.wait_ge(bias_mm, 1)
            V.tensor_copy(wb[:, :], bank[4][:, 1:2]).then_inc(wb_ready, 1)
            link(V.tensor_scalar(bsc[:, 6:7], bank[4][:, 0:1], MIN_SQ, None, ALU.max))
            inverse_root(bsc[:, 2:3], bsc[:, 6:7], 1, link)
            V.tensor_tensor(bsc[:, 1:2], bsc[:, 6:7], bsc[:, 2:3], ALU.mult).then_inc(fn_asked, 1)

            def stats(n):
                dve.wait_ge(x_loaded[n], 16)
                for t in range(8 * n, 8 * n + 8):
                    ins = V.bn_stats(st6[:, t, :], xm[:, t, :])
                link(ins)
                for t in range(8 * n, 8 * n + 8):
                    ins = V.bn_aggr(mv[:, t, :], st6[:, t, :])
                link(ins)
                cols = slice(8 * n, 8 * n + 8)
                link(V.tensor_scalar(row[0][:, cols], mv[:, cols, 1], LN_EPS, None, ALU.add))
                inverse_root(row[1][:, cols], row[0][:, cols], 8, link)

            def normalize(n):
                for t in range(8 * n, 8 * n + 8):
                    ins = V.tensor_scalar(xm[:, t, :], xm[:, t, :], mv[:, t, 0:1], row[1][:, t:t + 1],
                                          ALU.subtract, ALU.mult)
                    if t % 4 == 3:
                        ins.then_inc(xn_ready, 1)

            def sum_squares(g):
                dve.wait_ge(mx_squared, g + 1)
                V.tensor_reduce(row[3][:, 4 * g:4 * g + 4], sq[:, g % 2, :].rearrange("p (t d) -> p t d", d=D),
                                AX_X, ALU.add).then_inc(sq_used, 1)

            stats(0)
            stats(1)
            normalize(0)
            stats(2)
            normalize(1)
            dve.wait_ge(fn_done, 1)
            link(V.scalar_tensor_tensor(out=bsc[:, 4:5], in0=bsc[:, 3:4], scalar=MAX_NORM, in1=bsc[:, 2:3],
                                        op0=ALU.min, op1=ALU.mult))
            fac = bsc[:, 4:5]
            link(V.tensor_tensor(bsc[:, 5:6], fac, fac, ALU.mult))
            link(V.tensor_tensor(bsc[:, 5:6], bsc[:, 5:6], bank[4][:, 0:1], ALU.mult))
            y2 = bsc[:, 5:6]
            sum_squares(0)
            stats(3)
            normalize(2)
            sum_squares(1)
            sum_squares(2)
            normalize(3)
            for g in range(3, QUADS):
                sum_squares(g)

            def stt(o, a, s, b, op0, op1):
                return V.scalar_tensor_tensor(out=o, in0=a, scalar=s, in1=b, op0=op0, op1=op1)

            def artanh(o, a, ask):
                link(V.tensor_scalar(row[10], a, CLIP, None, ALU.min))
                V.tensor_scalar(row[11], row[10], 0.25, None, ALU.is_ge).then_inc(fn_asked, 1)
                link(V.tensor_tensor(row[16], row[10], row[10], ALU.mult))
                link(V.tensor_scalar(row[17], row[16], ATANH_SERIES[0], None, ALU.mult))
                for c in ATANH_SERIES[1:]:
                    link(stt(row[17], row[17], c, row[16], ALU.add, ALU.mult))
                link(stt(row[17], row[17], 1.0, row[10], ALU.add, ALU.mult))
                dve.wait_ge(fn_done, ask)
                link(V.tensor_tensor(row[12], row[12], row[13], ALU.subtract))
                link(stt(row[12], row[12], 0.5, row[17], ALU.mult, ALU.subtract))
                link(V.tensor_tensor(row[12], row[12], row[11], ALU.mult))
                link(V.tensor_tensor(o, row[12], row[17], ALU.add))

            link(V.tensor_tensor(row[2], row[1], row[1], ALU.mult))
            link(stt(row[2], row[2], float(D), mv[:, :, 1], ALU.mult, ALU.mult))
            V.tensor_scalar(row[4], row[2], MIN_SQ, None, ALU.max)
            dve.wait_ge(sq_used, QUADS)
            link(V.tensor_scalar(row[5], row[3], MIN_SQ, None, ALU.max))
            def rows_of(first, count):
                return sc[:, first:first + count, :].rearrange("p a t -> p (a t)")

            inverse_root(rows_of(8, 2), rows_of(4, 2), 2 * KT, link)
            link(V.tensor_tensor(rows_of(6, 2), rows_of(4, 2), rows_of(8, 2), ALU.mult))
            dve.wait_ge(xb_in_psum, 1)
            link(V.tensor_scalar(row[18], bank[7][:, 0:KT], fac, None, ALU.mult))
            artanh(row[19], row[6], 3)
            link(V.tensor_tensor(row[14], row[7], row[8], ALU.mult))
            V.tensor_tensor(row[14], row[14], row[19], ALU.mult).then_inc(fn_asked, 1)
            dve.wait_ge(fn_done, 4)
            link(V.tensor_scalar(row[15], row[15], MAX_NORM, None, ALU.min))
            link(V.tensor_tensor(row[9], row[15], row[9], ALU.mult))
            link(V.tensor_tensor(row[15], row[15], row[15], ALU.mult))
            link(V.tensor_tensor(row[14], row[18], row[9], ALU.mult))
            link(V.tensor_scalar(row[14], row[14], 2.0, 1.0, ALU.mult, ALU.add))
            link(stt(row[16], row[15], y2, row[14], ALU.mult, ALU.add))
            link(V.tensor_scalar(row[16], row[16], MIN_NORM, None, ALU.max))
            link(V.reciprocal(row[16], row[16]))
            link(stt(row[14], row[14], y2, row[16], ALU.add, ALU.mult))
            link(V.tensor_tensor(row[20], row[14], row[9], ALU.mult))
            link(V.tensor_scalar(row[15], row[15], -1.0, 1.0, ALU.mult, ALU.add))
            link(V.tensor_tensor(row[21], row[15], row[16], ALU.mult))
            link(V.tensor_tensor(row[14], row[20], row[3], ALU.mult))
            link(stt(row[15], row[21], 2.0, row[18], ALU.mult, ALU.mult))
            link(V.tensor_tensor(row[14], row[14], row[15], ALU.add))
            link(V.tensor_tensor(row[14], row[14], row[20], ALU.mult))
            link(stt(row[15], row[21], y2, row[21], ALU.mult, ALU.mult))
            link(V.tensor_tensor(row[14], row[14], row[15], ALU.add))
            link(V.tensor_scalar(row[4], row[14], MIN_SQ, None, ALU.max))
            inverse_root(row[8], row[4], KT, link)
            link(V.tensor_tensor(row[6], row[4], row[8], ALU.mult))
            link(V.tensor_scalar(row[19], row[6], MAX_NORM, None, ALU.min))
            artanh(row[19], row[19], 6)
            link(V.tensor_tensor(row[19], row[19], row[8], ALU.mult))
            link(stt(row[21], row[21], fac, row[19], ALU.mult, ALU.mult))
            V.tensor_tensor(row[20], row[20], row[19], ALU.mult).then_inc(gains_ready, 1)

            def split_lo(b, c):
                for h in range(SUBS):
                    at = (c * SUBS + h) % PART
                    dve.wait_ge(hi_made, b * HALVES + c * SUBS + h + 1)
                    V.tensor_tensor(adj_lo[:, at, :], raw_c[c % RAW][:, h * SW:(h + 1) * SW],
                                    adj_hi[:, at, :].bitcast(F32), ALU.subtract).then_inc(lo_made, 1)

            def sum_quad(g):
                dve.wait_ge(mx_scaled, g + 1)
                for t in range(4 * g, 4 * g + 4):
                    ins = stt(xm[:, t, :], b_bc[:, :], row[21][:, t:t + 1], xm[:, t, :], ALU.mult, ALU.add)
                ins.then_inc(xt_sum, 1)

            def lo_quad(g):
                dve.wait_ge(xt_hi_made, g + 1)
                quad = slice(4 * g, 4 * g + 4)
                V.tensor_tensor(xt_lo[:, quad, :], xm[:, quad, :], xt_hi[:, quad, :].bitcast(F32),
                                ALU.subtract).then_inc(xt_ready, 1)

            LINKS = 6

            def post(b, par, step):
                g = [ga[:, k, :] for k in range(16)]
                pair = [ga[:, k:k + 2, :].rearrange("p a q -> p (a q)") for k in range(0, 8, 2)]
                per_tile = lambda ap: ap.rearrange("p (q d) -> p q d", d=D)
                linked = [(0, 0, 5, 6)[step]]

                def chained(ins):
                    linked[0] += 1
                    ins.then_inc(ga_step, 1)
                    dve.wait_ge(ga_step, b * LINKS + linked[0])
                if step == 0:
                    wait(dve, ln_ready, b)
                    dve.wait_ge(rows_squared, b + 1)
                    V.tensor_reduce(g[0], per_tile(sq[:, 0, :]), AX_X, ALU.add).then_inc(sums_read, 1)
                    dve.wait_ge(relu_squared, b + 1)
                    V.tensor_reduce(g[1], per_tile(sq[:, 1, :]), AX_X, ALU.add).then_inc(sums_read, 1)
                    dve.wait_ge(sums_read, 2 * b + 2)
                    V.tensor_scalar(pair[1], pair[0], MIN_SQ, None, ALU.max).then_inc(norms_asked, 1)
                if step == 1:
                    dve.wait_ge(norms_rooted, b + 1)
                    chained(V.tensor_tensor(pair[3], pair[1], pair[2], ALU.mult))
                    chained(stt(g[8], g[6], ATANH_MAX, g[4], ALU.min, ALU.mult))
                    chained(V.tensor_tensor(g[9], g[7], g[8], ALU.mult))
                    chained(V.tensor_scalar(g[10], g[9], MIN_NORM, None, ALU.max))
                    V.reciprocal(g[12], g[10]).then_inc(tanh_asked, 1)
                    dve.wait_ge(tanh_asked, b + 1)
                    chained(V.tensor_tensor(g[13], g[8], g[12], ALU.mult))
                if step == 2:
                    dve.wait_ge(tanh_made, b + 1)
                    chained(stt(g[14], g[11], MAX_NORM, g[13], ALU.min, ALU.mult))
                    dve.wait_ge(xr_loaded[par], (b // 2 + 1) * 16 if isinstance(b, int) else (b - par) * 8 + 16)
                    for q in range(TILES):
                        V.scalar_tensor_tensor(out=xr[:, par, q, :], in0=rl[:, q * D:(q + 1) * D], scalar=ga[:, 14, q:q + 1],
                                               in1=xr[:, par, q, :], op0=ALU.mult, op1=ALU.add).then_inc(x2_ready, 1)
                    for q in range(TILES):
                        dve.wait_ge(x2_ready, b * TILES + q + 1)
                        ins = V.bn_stats(st6_b[:, q, :], xr[:, par, q, :])
                    ins.then_inc(stats_b, 1)
                    dve.wait_ge(stats_b, b + 1)
                if step == 3:
                    for q in range(TILES):
                        ins = V.bn_aggr(mv_b[:, q, :], st6_b[:, q, :])
                    ins.then_inc(mean_b, 1)
                    dve.wait_ge(mean_b, b + 1)
                    V.tensor_scalar(var_b[:, :, 0], mv_b[:, :, 1], LN_EPS, None, ALU.add).then_inc(var_ready, 1)

            def block_step(b, par):
                first = isinstance(b, int) and b == 0
                for c in range(CHUNKS):
                    if first:
                        sum_quad(c)
                        if c >= 1:
                            lo_quad(c - 1)
                        if c == CHUNKS - 1:
                            lo_quad(c)
                    split_lo(b, c)
                    if not first and c in DVE_POST_AT:
                        post(b - 1, 1 - par, DVE_POST_AT.index(c))
            blocks(dve, block_step)
            for step in range(4):
                post(BLOCKS - 1, 1, step)

            def relu_bias(layer, q, bank_n, dst, made):
                for k in range(KH):
                    at = k * HB + HID
                    V.tensor_scalar(dst[:, k * P:(k + 1) * P], bank[bank_n][:, k * P:(k + 1) * P],
                                    f_w[layer][q][:, at:at + 1], 0.0, ALU.add, ALU.max).then_inc(made, 1)

            def iteration(i, par):
                s, q = i - L1, par
                if live(s):
                    dve.wait_ge(l1_done, s + 1)
                    relu_bias(1, q, 4 * q + 2, f_h2[q], h2_made)
                s, q = i - L0, 1 - par
                if live(s):
                    dve.wait_ge(l0_done, s + 1)
                    relu_bias(0, q, 4 * q + 1, f_h1[q], h1_made)
                s, q = i - WO, 1 - par
                if live(s):
                    at = [dve.value_load(mint[0:1, 3 + g, bass.ds(s, 1)], min_val=0, max_val=TRASH + 3) for g in range(2)]
                    dve.wait_ge(wo_done, s + 1)
                    for g in range(2):
                        group = raw[:, bass.ds(at[g] * GR, GR)]
                        V.scalar_tensor_tensor(out=group, in0=bank[4 * q + 3][:, g * GR:(g + 1) * GR], scalar=bo_col[:, :],
                                               in1=group, op0=ALU.add, op1=ALU.add).then_inc(o_made, 1)
            dve.wait_ge(weff_made, LAYERS * KH)
            dve.wait_ge(meta_ready, 1)
            dve.wait_ge(x2t_loaded, 16)
            dve.wait_ge(turned_copied, 2 * BLOCKS)
            dve.wait_ge(trash_made, 1)
            pipeline(dve, iteration)

        @block.tensor
        def _(pe):
            T = nc.tensor
            pe.wait_ge(consts_made, 3)
            pe.wait_ge(even_ready, 1)
            T.matmul(bank[5][0:GROUPS, 0:1], rt[4], rc[:, 2:3], start=True, stop=True).then_inc(slot_mm, 1)
            pe.wait_ge(lead_ready, 1)
            for k, (col, h) in enumerate(((rc[:, 7:8], 0), (ones[0:GROUPS, 0:1], 0), (r_f[:, GROUPS:GROUPS + 1], 0),
                                          (rc[:, 7:8], 1), (ones[0:GROUPS, 0:1], 1))):
                mm = T.matmul(bank[6][0:1, k * SLOTS:(k + 1) * SLOTS], col, lead[:, h, :], start=True, stop=True)
            mm.then_inc(tables_mm, 1)
            pe.wait_ge(wload, 16 * WLOADS)
            pe.wait_ge(bsq_ready, 1)
            T.matmul(bank[4][:, 0:1], ones[:, :], bsc[:, 0:1], start=True, stop=True)
            T.matmul(bank[4][:, 1:2], w_sb, b_col[:, :], start=True, stop=True).then_inc(bias_mm, 1)

            def transpose_quad(g):
                pe.wait_ge(xn_ready, g + 1)
                if g >= 2:
                    pe.wait_ge(xnt_copied, g - 1)
                for q in range(4):
                    mm = T.transpose(bank[g % 2][:, q * P:(q + 1) * P], xm[:, 4 * g + q, :], ident[:, :])
                mm.then_inc(xnt_in_psum, 1)

            transpose_quad(0)
            pe.wait_ge(wb_ready, 1)
            for g in range(QUADS):
                if g + 1 < QUADS:
                    transpose_quad(g + 1)
                pe.wait_ge(xnt_copied, g + 1)
                if g >= 2:
                    pe.wait_ge(mx_squared, g - 1)
                for q in range(4):
                    xnt = work[:, g % 2, q * P:(q + 1) * P]
                    mb = T.matmul(bank[7][:, 4 * g + q:4 * g + q + 1], xnt, wb[:, :], start=True, stop=True)
                    mm = T.matmul(bank[2 + g % 2][:, q * P:(q + 1) * P], xnt, wt_sb, start=True, stop=True)
                if g == QUADS - 1:
                    mb.then_inc(xb_in_psum, 1)
                mm.then_inc(mx_in_psum, 1)

            def rows_of_block(b, par):
                pe.wait_ge(support_copied, b + 1)
                wait(pe, relu_made, b - 1)
                for q in range(TILES):
                    mm = T.transpose(bank[2 + par][:, q * P:(q + 1) * P], work[:, par, q * P:(q + 1) * P], ident[:, :])
                mm.then_inc(rows_ready, 1)

            def turn(b, par):
                pe.wait_ge(ln_ready, b + 1)
                wait(pe, turned_copied, 2 * b)
                for q in range(TILES):
                    T.transpose(bank[4][:, q * P:(q + 1) * P], rl[:, q * P:(q + 1) * P], ident[:, :])
                    mm = T.transpose(bank[6][:, q * P:(q + 1) * P], xr[:, par, q, :], ident[:, :])
                mm.then_inc(turned, 1)

            def block_step(b, par):
                first = isinstance(b, int) and b == 0
                wait(pe, support_copied, b - 1)
                for c in range(CHUNKS):
                    if first:
                        pe.wait_ge(xt_ready, c + 1)
                    for k in range(CK):
                        t = c * CK + k
                        half, k_in = c * SUBS + k // SK, k % SK
                        if k_in == 0:
                            pe.wait_ge(lo_made, b * HALVES + half + 1)
                        hi = adj_hi[:, half % PART, k_in * ROWS:(k_in + 1) * ROWS]
                        lo = adj_lo[:, half % PART, k_in * ROWS:(k_in + 1) * ROWS]
                        T.matmul(bank[par][:, :], xt_hi[:, t, :], hi, start=(t == 0), stop=False)
                        T.matmul(bank[par][:, :], xt_hi[:, t, :], lo, start=False, stop=False)
                        mm = T.matmul(bank[par][:, :], xt_lo[:, t, :], hi, start=False, stop=(t == KT - 1))
                        if k_in == SK - 1:
                            mm.then_inc(half_used, 1)
                    if c == CHUNKS - 1:
                        T.matmul(bank[5][:, 0:1], ident[:, :], ones[:, 0:1], start=True, stop=True).then_inc(support_ready, 1)
                    if not first and c == 2:
                        rows_of_block(b - 1, 1 - par)
                    if c == 0 and not (isinstance(b, int) and b < 2):
                        turn(b - 2, par)
            blocks(pe, block_step)
            turn(BLOCKS - 2, 0)
            rows_of_block(BLOCKS - 1, 1)
            turn(BLOCKS - 1, 1)

            def routed(w, h, sums, done):
                for m in range(KH):
                    for k in range(KH):
                        mm = T.matmul(sums[:, m * P:(m + 1) * P], w[:, k * HB + m * P:k * HB + (m + 1) * P],
                                      h[:, k * P:(k + 1) * P], start=(k == 0), stop=(k == KH - 1))
                mm.then_inc(done, 1)

            def iteration(i, par):
                s, q = i - WO, 1 - par
                if live(s):
                    pe.wait_ge(h2_made, KH * s + KH)
                    wait(pe, o_made, 2 * s - 2)
                    for k in range(KH):
                        mm = T.matmul(bank[4 * q + 3][:, 0:P], wo_sb[:, k, :], f_h2[q][:, k * P:(k + 1) * P],
                                      start=(k == 0), stop=(k == KH - 1))
                    mm.then_inc(wo_done, 1)
                s, q = i - L1, par
                if live(s):
                    pe.wait_ge(h1_made, KH * s + KH)
                    pe.wait_ge(w_copied[1], s + 1)
                    routed(f_w[1][q], f_h1[q], bank[4 * q + 2], l1_done)
                s, q = i - L0, 1 - par
                if live(s):
                    pe.wait_ge(h0_made, KH * s + KH)
                    pe.wait_ge(w_copied[0], s + 1)
                    routed(f_w[0][q], f_h0[q], bank[4 * q + 1], l0_done)
                s, q = i - WI, par
                if live(s):
                    pe.wait_ge(gathered, 2 * s + 2)
                    for k in range(KH):
                        mm = T.matmul(bank[4 * q][:, k * P:(k + 1) * P], wi_sb[:, k * P:(k + 1) * P], f_xt[q],
                                      start=True, stop=True)
                    mm.then_inc(wi_done, 1)
            pe.wait_ge(meta_ready, 1)
            pe.wait_ge(weff_made, LAYERS * KH)
            pe.wait_ge(turned_copied, 2 * BLOCKS)
            pipeline(pe, iteration)


def kernel(**inputs):
    import concourse.bacc as bacc
    from concourse.bass_utils import run_bass_kernel_spmd as run

    nc = bacc.Bacc("TRN2", target_bir_lowering=False, num_devices=1)
    arrays = {}

    def dram(name, a):
        a = np.ascontiguousarray(a)
        arrays[name] = a
        return nc.dram_tensor(name, a.shape, mybir.dt.from_np(a.dtype), kind="ExternalInput").ap()

    def get(name):
        return np.asarray(inputs[name])

    def by_partition(a):
        n = a.shape[1]
        a = a.transpose(0, 3, 1, 2).reshape(LAYERS, KH, P, n, HID)
        return a.transpose(2, 0, 1, 3, 4).reshape(P, LAYERS * KH, n, HID)

    def bias_by_partition(a):
        n = a.shape[1]
        return a.reshape(LAYERS, n, KH, P).transpose(3, 0, 2, 1).reshape(P, LAYERS * KH, n)

    def with_bias(weights, biases):
        return np.concatenate([by_partition(get(weights)), bias_by_partition(get(biases))[..., None]], axis=3)

    w = get("L0_gnn_weight")
    args = [
        dram("x", get("x")),
        dram("adj_t", get("adj").reshape(BLOCKS, ROWS, P, KT).transpose(0, 2, 3, 1).reshape(BLOCKS, P, KT * ROWS)),
        dram("w", w),
        dram("w_t", w.T),
        dram("bias", get("L0_gnn_bias")),
        dram("route", get("L0_ffn_route_id")),
        dram("wi_t", get("L0_ffn_Wi").T),
        dram("bi", get("L0_ffn_bi").reshape(KH, P).T),
        dram("wr_t", with_bias("L0_ffn_Wr", "L0_ffn_br")),
        dram("ws_t", with_bias("L0_ffn_Ws", "L0_ffn_bs")[:, :, 0, :]),
        dram("wo_t", get("L0_ffn_Wo").T.reshape(KH, P, D).transpose(1, 0, 2)),
        dram("bo", get("L0_ffn_bo")),
        nc.dram_tensor("x2t_dram", (D, N), F32, kind="Internal").ap(),
        nc.dram_tensor("out_t", (D, N), F32, kind="ExternalOutput").ap(),
    ]
    build(nc, *args)
    r = run(nc, [arrays], core_ids=[0])
    return r.results[0]["out_t"].T
```

```python
from contextlib import ExitStack

import numpy as np

import concourse.bass as bass
from concourse import mybir

F32 = mybir.dt.float32
F32R = mybir.dt.float32r
I32 = mybir.dt.int32
ALU = mybir.AluOpType
ACT = mybir.ActivationFunctionType
AX_X = mybir.AxisListType.X

P = 128
N = 4096
D = 128
HID = 256
KT = N // P
ROWS = 512
BLOCKS = N // ROWS
TILES = ROWS // P
CK = 4
CHUNKS = KT // CK
CW = CK * ROWS
RAW = 4
SUBS = 2
PART = 4
SW = CW // SUBS
SK = CK // SUBS
HALVES = CHUNKS * SUBS
EARLY = PART // SUBS

LAYERS, EXPERTS = 2, 16
E1 = EXPERTS + 1
GROUPS = 64
GR = N // GROUPS
SLOTS = (GROUPS + E1) // 2
KH = HID // P
HB = HID + 1

MIN_NORM = 1e-15
MIN_SQ = 1e-30
MAX_NORM = float(np.float32(1.0 - 1e-5))
CLIP = float(np.float32(1.0 - 1e-7))
ATANH_MAX = float(np.arctanh(np.float64(np.float32(1.0 - 1e-5))))
LN_EPS = 1e-5
ATANH_SERIES = [1.0 / 13, 1.0 / 11, 1.0 / 9, 1.0 / 7, 1.0 / 5, 1.0 / 3]

GATHER, COPY, WI, L0, L1, WO = -1, (-1, 0), 0, 1, 2, 3
HEAD = range(GATHER, 8)
BODY = (8, SLOTS - 4)
UNROLL = 4
TAIL = range(SLOTS - 4, SLOTS + WO)
POST_AT = [1, 4, 6]
DVE_POST_AT = [4, 5, 6, 7]
FINAL_AT = 2


def build(nc, x, adj_t, w, bias, route, wi_t, bi, wr_t, ws_t, wo_t, bo, x2t_dram, out_t):
    with ExitStack() as ctx:
        def sb(name, shape, dt=F32):
            return ctx.enter_context(nc.sbuf_tensor(name, shape, dt))

        def sem(name):
            return ctx.enter_context(nc.semaphore(name))

        pairs = [ctx.enter_context(nc.psum_tensor(f"banks{2 * i}{2 * i + 1}", [P, 2, 512], F32)) for i in range(4)]
        bank = [pairs[i // 2][:, i % 2, :] for i in range(8)]

        xm = sb("xm", [P, KT, D])
        xt_hi = sb("xt_hi", [P, KT, D], F32R)
        xt_lo = sb("xt_lo", [P, KT, D], F32R)
        raw = sb("raw", [P, RAW * CW])
        adj_hi = sb("adj_hi", [P, PART, SW], F32R)
        adj_lo = sb("adj_lo", [P, PART, SW], F32R)
        weff = sb("weff", [P, LAYERS * KH, E1, HB])
        wi_sb = sb("wi_sb", [P, HID])
        bi_sb = sb("bi_sb", [P, KH])
        wo_sb = sb("wo_sb", [P, KH, D])
        bo_col = sb("bo_col", [P, 1])
        b_col = sb("b_col", [P, 1])
        b_bc = sb("b_bc", [P, D])
        ident = sb("ident", [P, P])
        ones = sb("ones", [P, P])
        work = sb("work", [P, 2, 512])
        sq = sb("sq", [P, 2, 512])
        rl = sb("rl", [P, 512])
        xr = sb("xr", [P, 2, TILES, D])
        st6 = sb("st6", [P, KT, 6])
        mv = sb("mv", [P, KT, 2])
        w_mean = sb("w_mean", [P, 1])
        sc = sb("sc", [P, 22, KT])
        row = [sc[:, n, :] for n in range(22)]
        bsc = sb("bsc", [P, 8])
        tmp_i = sb("tmp_i", [P, 3 * KT], I32)
        f_expo = sb("f_expo", [P, 1])
        ga = sb("ga", [P, 16, TILES])
        x2t_out = sb("x2t_out", [P, ROWS])
        w_sb, wt_sb = x2t_out[:, 0:D], x2t_out[:, D:2 * D + 1]
        AT = 2 * D + 1
        st6_b = sb("st6_b", [P, TILES, 6])
        mv_b = sb("mv_b", [P, TILES, 2])
        var_b = sb("var_b", [P, TILES, 1])
        rstd_b = sb("rstd_b", [P, TILES, 1])
        r_int = sb("r_int", [GROUPS, GROUPS + 1], I32)
        r_f = sb("r_f", [GROUPS, GROUPS + 1])
        valid = sb("valid", [GROUPS, GROUPS + 1])
        later = rl[0:GROUPS, 0:GROUPS]
        earlier = rl[0:GROUPS, GROUPS:2 * GROUPS]
        rt = [rl[0:GROUPS, (2 + n) * GROUPS:(3 + n) * GROUPS] for n in range(5)]
        rc = sb("rc", [GROUPS, 8])
        rci = sb("rci", [GROUPS, 2], I32)
        iota_f = x2t_out[0:GROUPS, AT:AT + SLOTS]
        tmp_f = x2t_out[:, AT + 3 * SLOTS:AT + 3 * SLOTS + 3 * KT]
        lead = x2t_out[0:GROUPS, AT + SLOTS:AT + 3 * SLOTS].rearrange("p (a s) -> p a s", a=2)
        mrow = sb("mrow", [1, 8, SLOTS])
        trash = sb("trash", [1, SLOTS // 2, 2])
        mint = sb("mint", [1, 5, SLOTS], I32)
        xnt = xm[:, :, :].rearrange("p t d -> p (t d)")
        TRASH = GROUPS
        RINGS = (GROUPS + 4) * GR

        def ring(at, width):
            return [raw[:, RINGS + at + n * width:RINGS + at + (n + 1) * width] for n in range(2)]

        f_xt = [work[:, n, 0:P] for n in range(2)]
        f_w = [ring(6 * HID + layer * 2 * KH * HB, KH * HB) for layer in range(LAYERS)]
        f_h0, f_h1, f_h2 = (ring(n * 2 * HID, HID) for n in range(3))

        square = sq[:, :, :].rearrange("p a (t d) -> p (a t) d", d=D)
        mx_pair = [pairs[1 + n][:, :, 0:2 * (D + 1)].rearrange("p a (t d) -> p a t d", t=2) for n in range(2)]

        x_loaded = [sem(f"x_loaded{n}") for n in range(4)]
        w_loaded = sem("w_loaded")
        wload = sem("wload")
        route_loaded = sem("route_loaded")
        wr_loaded = [sem(f"wr_loaded{lk}") for lk in range(LAYERS * KH)]
        pool_step = sem("pool_step")
        consts_made = sem("consts_made")
        dve_step = sem("dve_step")
        even_ready = sem("even_ready")
        slot_mm = sem("slot_mm")
        lead_ready = sem("lead_ready")
        tables_mm = sem("tables_mm")
        meta_ready = sem("meta_ready")
        w_centred = sem("w_centred")
        w_turned = sem("w_turned")
        wt_ready = sem("wt_ready")
        stats_made = sem("stats_made")
        x_in_psum = sem("x_in_psum")
        x_turned = sem("x_turned")
        mx_in_psum = sem("mx_in_psum")
        mx_copied = sem("mx_copied")
        mx_squared = sem("mx_squared")
        squares_summed = sem("squares_summed")
        bias_asked = sem("bias_asked")
        bias_tanh = sem("bias_tanh")
        fn_asked = sem("fn_asked")
        fn_done = sem("fn_done")
        gains_ready = sem("gains_ready")
        mx_scaled = sem("mx_scaled")
        xt_sum = sem("xt_sum")
        xt_hi_made = sem("xt_hi_made")
        xt_ready = sem("xt_ready")
        adj_loaded = [sem(f"adj_loaded{n}") for n in range(RAW)]
        hi_made = sem("hi_made")
        lo_made = sem("lo_made")
        half_used = sem("half_used")
        support_ready = sem("support_ready")
        support_copied = sem("support_copied")
        rows_ready = sem("rows_ready")
        rows_squared = sem("rows_squared")
        relu_made = sem("relu_made")
        relu_squared = sem("relu_squared")
        sums_read = sem("sums_read")
        tanh_asked = sem("tanh_asked")
        tanh_made = sem("tanh_made")
        ga_step = sem("ga_step")
        xr_loaded = [sem(f"xr_loaded{n}") for n in range(2)]
        x2_ready = sem("x2_ready")
        norms_asked = sem("norms_asked")
        norms_rooted = sem("norms_rooted")
        stats_b = sem("stats_b")
        mean_b = sem("mean_b")
        var_ready = sem("var_ready")
        rstd_ready = sem("rstd_ready")
        centred = sem("centred")
        ln_ready = sem("ln_ready")
        turned = sem("turned")
        turned_copied = sem("turned_copied")
        x2t_stored = sem("x2t_stored")
        last_x2t_stored = sem("last_x2t_stored")
        x2t_loaded = sem("x2t_loaded")
        weff_made = sem("weff_made")
        trash_made = sem("trash_made")
        gathered = sem("gathered")
        wi_done = sem("wi_done")
        h0_made = sem("h0_made")
        w_copied = [sem(f"w_copied{layer}") for layer in range(LAYERS)]
        l0_done = sem("l0_done")
        h1_made = sem("h1_made")
        l1_done = sem("l1_done")
        h2_made = sem("h2_made")
        wo_done = sem("wo_done")
        o_made = sem("o_made")
        o_stored = [sem(f"o_stored{n}") for n in range(2)]

        def wait(eng, semaphore, value):
            if isinstance(value, int) and value <= 0:
                return
            eng.wait_ge(semaphore, value)

        def blocks(eng, block_step, peeled=2):
            for b in range(peeled):
                block_step(b, b % 2)
            with eng.Fori(peeled // 2, BLOCKS // 2) as pair:
                block_step(pair * 2, 0)
                block_step(pair * 2 + 1, 1)

        def pipeline(eng, iteration):
            for i in HEAD:
                iteration(i, i % 2)
            with eng.Fori(BODY[0] // UNROLL, BODY[1] // UNROLL) as quad:
                for n in range(UNROLL):
                    iteration(quad * UNROLL + n, n % 2)
            for i in TAIL:
                iteration(i, i % 2)

        def live(slot):
            return not isinstance(slot, int) or 0 <= slot < SLOTS

        raw_c = [raw[:, r * CW:(r + 1) * CW] for r in range(RAW)]
        WLOADS = 6
        QUADS = KT // 4
        SQUARES_ON_ACT = 4

        block = ctx.enter_context(nc.Block())

        @block.sync
        def _(sp):
            sp.dma_start(r_int[:, 0:GROUPS], route.rearrange("(a n) -> a n", a=1).to_broadcast([GROUPS, GROUPS])).then_inc(route_loaded, 16)
            sp.dma_start(r_int[:, GROUPS:GROUPS + 1], route.rearrange("(n a) -> n a", a=1)).then_inc(route_loaded, 16)
            sp.dma_start(w_sb, w).then_inc(w_loaded, 16)
            sp.dma_start(b_col[:, :], bias.rearrange("(p a) -> p a", a=1)).then_inc(w_loaded, 16)
            for n in range(4):
                sp.dma_start(xm[:, n * 8:(n + 1) * 8, :],
                             x.rearrange("(p t) d -> p t d", p=P)[:, n * 8:(n + 1) * 8, :]).then_inc(x_loaded[n], 16)
            sp.dma_start(b_bc[:, :], bias.rearrange("(a n) -> a n", a=1).to_broadcast([P, D])).then_inc(wload, 16)
            sp.dma_start(wi_sb[:, :], wi_t).then_inc(wload, 16)
            sp.dma_start(bi_sb[:, :], bi).then_inc(wload, 16)
            sp.dma_start(wo_sb[:, :, :], wo_t).then_inc(wload, 16)
            sp.dma_start(bo_col[:, :], bo.rearrange("(p a) -> p a", a=1)).then_inc(wload, 16)
            sp.dma_start(weff[:, :, EXPERTS, :], ws_t).then_inc(wload, 16)
            for c in range(RAW):
                if c == EARLY:
                    for lk in range(KH):
                        sp.dma_start(weff[:, lk, 0:EXPERTS, :], wr_t[:, lk, :, :]).then_inc(wr_loaded[lk], 16)
                sp.dma_start(raw_c[c], adj_t[0, :, c * CW:(c + 1) * CW]).then_inc(adj_loaded[c], 16)
            for lk in range(KH, LAYERS * KH):
                sp.dma_start(weff[:, lk, 0:EXPERTS, :], wr_t[:, lk, :, :]).then_inc(wr_loaded[lk], 16)

            def load_block(b, par):
                for c in range(CHUNKS):
                    if isinstance(b, int) and b * CHUNKS + c < RAW:
                        continue
                    sp.wait_ge(lo_made, (b * CHUNKS + c - RAW + 1) * SUBS)
                    sp.dma_start(raw_c[c % RAW], adj_t[bass.ds(b, 1), :, c * CW:(c + 1) * CW].rearrange("a p n -> (a p) n")
                                 ).then_inc(adj_loaded[c % RAW], 16)
            blocks(sp, load_block)

            sp.wait_ge(turned_copied, 2 * BLOCKS - 2)
            sp.dma_start(x2t_dram[:, N - 2 * ROWS:N - ROWS], x2t_out[:, :]).then_inc(last_x2t_stored, 16)
            sp.wait_ge(x2t_stored, (BLOCKS - 2) * 16)
            sp.wait_ge(last_x2t_stored, 16)
            sp.wait_ge(lo_made, BLOCKS * HALVES)
            kept = N - ROWS
            sp.dma_start(raw[:, 0:kept], x2t_dram[:, 0:kept]).then_inc(x2t_loaded, 16)

            sp.wait_ge(meta_ready, 1)

            def iteration(i, par):
                s = i - WO
                if live(s):
                    at = [sp.value_load(mint[0:1, 3 + g, bass.ds(s, 1)], min_val=0, max_val=TRASH + 3) for g in range(2)]
                    sp.wait_ge(o_made, 2 * s + 2)
                    for g in range(2):
                        sp.dma_start(out_t[bass.ds(at[g], 1), :, :].rearrange("a d n -> (a d) n"),
                                     raw[:, bass.ds(at[g] * GR, GR)]).then_inc(o_stored[1 - par], 16)
            pipeline(sp, iteration)
            for q in range(2):
                sp.wait_ge(o_stored[q], SLOTS // 2 * 32)

        @block.gpsimd
        def _(pool):
            steps = 0
            for dst, val in ((ident[:, :], 0.0), (ones[:, :], 1.0), (later, 1.0), (earlier, 1.0),
                             (f_expo[:, :], -0.5)):
                nc.gpsimd.memset(dst, val).then_inc(pool_step, 1)
                steps += 1
            nc.gpsimd.iota(iota_f[:, :], pattern=[[1, SLOTS]], base=0, channel_multiplier=0,
                           allow_small_or_imprecise_dtypes=True).then_inc(pool_step, 1)
            nc.gpsimd.iota(rc[:, 7:8], pattern=[[0, 1]], base=0, channel_multiplier=1,
                           allow_small_or_imprecise_dtypes=True).then_inc(pool_step, 1)
            steps += 2
            pool.wait_ge(pool_step, steps)
            nc.gpsimd.affine_select(out=ident[:, :], in_=ident[:, :], compare_op=ALU.not_equal, fill=1.0, base=0,
                                    pattern=[[-1, P]], channel_multiplier=1).then_inc(consts_made, 1)
            nc.gpsimd.affine_select(out=later, in_=later, compare_op=ALU.is_gt, fill=0.0, base=0,
                                    pattern=[[1, GROUPS]], channel_multiplier=-1).then_inc(consts_made, 1)
            nc.gpsimd.affine_select(out=earlier, in_=earlier, compare_op=ALU.is_gt, fill=0.0, base=0,
                                    pattern=[[-1, GROUPS]], channel_multiplier=1).then_inc(consts_made, 1)

            pool.dma_start(xr[:, 0, :, :], x[0:ROWS, :].rearrange("(q p) d -> p q d", p=P)).then_inc(xr_loaded[0], 16)

            def make_weff(lk, part):
                if part == 0:
                    pool.wait_ge(wr_loaded[lk], 16)
                    diag = weff[:, lk, EXPERTS, (lk % KH) * P:(lk % KH + 1) * P]
                    nc.gpsimd.tensor_tensor(diag, diag, ident[:, :], ALU.add).then_inc(pool_step, 1)
                    pool.wait_ge(pool_step, steps + lk + 1)
                half = EXPERTS // 2
                experts = weff[:, lk, part * half:(part + 1) * half, :]
                nc.gpsimd.tensor_tensor(experts, experts, weff[:, lk, EXPERTS:E1, :].to_broadcast([P, half, HB]),
                                        ALU.add).then_inc(weff_made, 1)

            pool.wait_ge(consts_made, 3)
            pool.wait_ge(wload, 16 * WLOADS)
            make_weff(0, 0)
            make_weff(0, 1)

            for half in range(EARLY * SUBS):
                c, h = half // SUBS, half % SUBS
                pool.wait_ge(hi_made, half + 1)
                nc.gpsimd.tensor_tensor(adj_lo[:, half, :], raw_c[c][:, h * SW:(h + 1) * SW],
                                        adj_hi[:, half, :].bitcast(F32), ALU.subtract).then_inc(lo_made, 1)

            def scale_quad(g):
                quad = slice(4 * g, 4 * g + 4)
                nc.gpsimd.tensor_tensor(xm[:, quad, :], xm[:, quad, :],
                                        row[20][:, quad].rearrange("p (t a) -> p t a", a=1).to_broadcast([P, 4, D]),
                                        ALU.mult).then_inc(mx_scaled, 1)

            pool.wait_ge(gains_ready, 1)
            pool.wait_ge(mx_copied, 2 * QUADS)
            scale_quad(0)
            scale_quad(1)
            for g in range(QUADS):
                if g + 2 < QUADS:
                    scale_quad(g + 2)
                quad = slice(4 * g, 4 * g + 4)
                pool.wait_ge(xt_hi_made, g + 1)
                nc.gpsimd.tensor_tensor(xt_lo[:, quad, :], xm[:, quad, :], xt_hi[:, quad, :].bitcast(F32),
                                        ALU.subtract).then_inc(xt_ready, 1)

            make_weff(1, 0)
            make_weff(1, 1)
            make_weff(2, 0)

            expo = f_expo[:, :].to_broadcast([P, 2 * TILES])
            expo_b = f_expo[:, :].rearrange("p (a n) -> p a n", a=1).to_broadcast([P, TILES, 1])

            def block_step(b, par, last=False):
                if not last:
                    wait(pool, turned, 2 * b)
                    pool.dma_start(xr[:, 1 - par, :, :], x[bass.ds(b * ROWS + ROWS, ROWS), :].rearrange("(q p) d -> p q d", p=P)
                                   ).then_inc(xr_loaded[1 - par], 16)
                pool.wait_ge(norms_asked, b + 1)
                nc.gpsimd.tensor_tensor(ga[:, 4:6, :].rearrange("p a q -> p (a q)"), ga[:, 2:4, :].rearrange("p a q -> p (a q)"),
                                        expo, ALU.pow).then_inc(norms_rooted, 1)
                if isinstance(b, int) and b < 2:
                    make_weff(2 + b, 1)
                pool.wait_ge(var_ready, b + 1)
                nc.gpsimd.tensor_tensor(rstd_b[:, :, :], var_b[:, :, :], expo_b, ALU.pow).then_inc(rstd_ready, 1)
                if last:
                    return
                rows = rl[:, :].rearrange("p (q d) -> p q d", d=D)
                nc.gpsimd.tensor_tensor(rows, xr[:, par, :, :], mv_b[:, :, 0:1].to_broadcast([P, TILES, D]),
                                        ALU.subtract).then_inc(centred, 1)
                pool.wait_ge(rstd_ready, b + 1)
                pool.wait_ge(centred, b + 1)
                nc.gpsimd.tensor_tensor(rows, rows, rstd_b[:, :, :].to_broadcast([P, TILES, D]), ALU.mult).then_inc(ln_ready, 1)
                if isinstance(b, int) and b == BLOCKS - 2:
                    return
                pool.wait_ge(turned_copied, 2 * b + 2)
                pool.dma_start(x2t_dram[:, bass.ds(b * ROWS, ROWS)], x2t_out[:, :]).then_inc(x2t_stored, 16)
                if isinstance(b, int) and b == 0:
                    make_weff(3, 0)

            block_step(0, 0)
            block_step(1, 1)
            with pool.Fori(1, BLOCKS // 2 - 1) as pair:
                block_step(pair * 2, 0)
                block_step(pair * 2 + 1, 1)
            block_step(BLOCKS - 2, 0)
            block_step(BLOCKS - 1, 1, last=True)

            pool.wait_ge(lo_made, BLOCKS * HALVES)
            nc.gpsimd.memset(raw[:, TRASH * GR:(TRASH + 4) * GR], 0.0).then_inc(trash_made, 1)
            pool.wait_ge(meta_ready, 1)

            def iteration(i, par):
                s, q = i - GATHER, 1 - par
                if live(s):
                    src = []
                    for g in range(2):
                        if g == 1:
                            wait(pool, wi_done, s - 1)
                        src.append(pool.value_load(mint[0:1, g, bass.ds(s, 1)], min_val=0, max_val=GROUPS - 1))
                    if isinstance(s, int) and s == 0:
                        pool.wait_ge(turned_copied, 2 * BLOCKS - 1)
                    for g in range(2):
                        nc.gpsimd.tensor_copy(f_xt[q][:, g * GR:(g + 1) * GR], xnt[:, bass.ds(src[g] * GR, GR)]).then_inc(gathered, 1)
            pipeline(pool, iteration)

        @block.scalar
        def _(act):
            act.wait_ge(w_turned, 1)
            nc.scalar.activation(wt_sb, bank[7][:, 0:D + 1], ACT.Copy).then_inc(wt_ready, 1)

            def copy_x(g):
                act.wait_ge(x_in_psum, g + 1)
                if g >= 2:
                    act.wait_ge(mx_in_psum, g - 1)
                nc.scalar.activation(work[:, g % 2, :], bank[g % 2], ACT.Copy).then_inc(x_turned, 1)

            copy_x(0)
            for g in range(QUADS):
                if g + 1 < QUADS:
                    copy_x(g + 1)
                act.wait_ge(mx_in_psum, g + 1)
                mx = mx_pair[g % 2]
                act.wait_ge(stats_made, 4 * g + 4)
                nc.scalar.activation(xm[:, 4 * g:4 * g + 4, :].rearrange("p (a t) d -> p a t d", a=2), mx[:, :, :, 0:D],
                                     ACT.Copy).then_inc(mx_copied, 1)
                nc.scalar.activation(row[18][:, 4 * g:4 * g + 4].rearrange("p (a t) -> p a t", a=2), mx[:, :, :, D],
                                     ACT.Copy).then_inc(mx_copied, 1)
                if g >= SQUARES_ON_ACT:
                    if g >= SQUARES_ON_ACT + 2:
                        act.wait_ge(squares_summed, g - SQUARES_ON_ACT - 1)
                    nc.scalar.activation(sq[:, g % 2, :].rearrange("p (a t d) -> p a t d", a=2, t=2), mx[:, :, :, 0:D],
                                         ACT.Square).then_inc(mx_squared, 1)
                    continue
                for q in range(4):
                    t = 4 * g + q
                    mm = nc.scalar.activation(square[:, t % 8, :], mx[:, q // 2, q % 2, 0:D], ACT.Square,
                                              accum_out=row[3][:, t:t + 1])
                mm.then_inc(mx_squared, 1)

            def logs(asked):
                act.wait_ge(fn_asked, asked)
                nc.scalar.activation(row[12], row[10], ACT.Ln, bias=1.0).then_inc(fn_done, 1)
                nc.scalar.activation(row[13], row[10], ACT.Ln, bias=1.0, scale=-1.0).then_inc(fn_done, 1)

            def split_hi_early(c):
                act.wait_ge(adj_loaded[c], 16)
                for h in range(SUBS):
                    nc.scalar.activation(adj_hi[:, c * SUBS + h, :], raw_c[c][:, h * SW:(h + 1) * SW], ACT.Copy).then_inc(hi_made, 1)

            logs(1)
            act.wait_ge(bias_asked, 1)
            nc.scalar.activation(bsc[:, 3:4], bsc[:, 1:2], ACT.Tanh).then_inc(bias_tanh, 1)
            split_hi_early(0)
            act.wait_ge(fn_asked, 2)
            nc.scalar.activation(row[15], row[14], ACT.Tanh).then_inc(fn_done, 1)
            for c in range(1, EARLY):
                split_hi_early(c)
            logs(3)
            act.wait_ge(gains_ready, 1)

            def split_hi(b, c):
                if isinstance(b, int) and b == 0 and c < EARLY:
                    return
                act.wait_ge(adj_loaded[c % RAW], b * (CHUNKS // RAW * 16) + (c // RAW + 1) * 16)
                for h in range(SUBS):
                    wait(act, half_used, b * HALVES + c * SUBS + h - PART + 1)
                    nc.scalar.activation(adj_hi[:, (c * SUBS + h) % PART, :], raw_c[c % RAW][:, h * SW:(h + 1) * SW],
                                         ACT.Copy).then_inc(hi_made, 1)

            def hi_quad(g):
                act.wait_ge(xt_sum, g + 1)
                nc.scalar.activation(xt_hi[:, 4 * g:4 * g + 4, :], xm[:, 4 * g:4 * g + 4, :], ACT.Copy).then_inc(xt_hi_made, 1)

            def post(b, par, step, positive=rl[:, :]):
                rows = bank[2 + par][:, :]
                if step == 0:
                    act.wait_ge(support_ready, b + 1)
                    nc.scalar.activation(work[:, par, :], bank[par][:, :], ACT.Copy).then_inc(support_copied, 1)
                if step == 1:
                    act.wait_ge(rows_ready, b + 1)
                    wait(act, sums_read, 2 * b)
                    nc.scalar.activation(sq[:, 0, :], rows, ACT.Square).then_inc(rows_squared, 1)
                    wait(act, x2_ready, b * TILES)
                    nc.scalar.activation(positive, rows, ACT.Relu).then_inc(relu_made, 1)
                    act.wait_ge(relu_made, b + 1)
                    nc.scalar.activation(sq[:, 1, :], positive, ACT.Square).then_inc(relu_squared, 1)
                if step == 2:
                    act.wait_ge(tanh_asked, b + 1)
                    nc.scalar.activation(ga[:, 11, :], ga[:, 10, :], ACT.Tanh).then_inc(tanh_made, 1)

            def final(b):
                act.wait_ge(turned, 2 * b + 2)
                wait(act, x2t_stored, b * 16)
                nc.scalar.activation(x2t_out[:, :], bank[6], ACT.Copy).then_inc(turned_copied, 1)
                nc.scalar.activation(xnt[:, bass.ds(b * ROWS, ROWS)], bank[4], ACT.Copy).then_inc(turned_copied, 1)

            def block_step(b, par):
                first = isinstance(b, int) and b == 0
                for c in range(CHUNKS):
                    if first:
                        hi_quad(c)
                    split_hi(b, c)
                    if not first and c in POST_AT:
                        post(b - 1, 1 - par, POST_AT.index(c))
                    if c == FINAL_AT and not (isinstance(b, int) and b < 2):
                        final(b - 2)
            blocks(act, block_step, peeled=4)
            post(BLOCKS - 1, 1, 0)
            post(BLOCKS - 1, 1, 1, work[:, 0, :])
            final(BLOCKS - 2)
            post(BLOCKS - 1, 1, 2)
            act.wait_ge(turned, 2 * BLOCKS - 1)
            nc.scalar.activation(xnt[:, N - ROWS:N], bank[4], ACT.Copy).then_inc(turned_copied, 1)
            act.wait_ge(turned, 2 * BLOCKS)
            act.wait_ge(lo_made, BLOCKS * HALVES)
            nc.scalar.activation(raw[:, N - ROWS:N], bank[6], ACT.Copy).then_inc(turned_copied, 1)

            def ready_to_copy(i):
                if live(i - 1):
                    act.wait_ge(h1_made, KH * i)
                elif live(i - 2):
                    act.wait_ge(h2_made, KH * i - KH)

            def iteration(i, par):
                s, q = i - WI, par
                if live(s):
                    act.wait_ge(wi_done, s + 1)
                    for k in range(KH):
                        if k == KH - 1:
                            ready_to_copy(i)
                        nc.scalar.activation(f_h0[q][:, k * P:(k + 1) * P], bank[4 * q][:, k * P:(k + 1) * P], ACT.Relu,
                                             bias=bi_sb[:, k:k + 1]).then_inc(h0_made, 1)
                else:
                    ready_to_copy(i)
                for layer in range(LAYERS):
                    s = i - COPY[layer]
                    q = (par - COPY[layer]) % 2
                    if live(s):
                        e = act.value_load(mint[0:1, 2, bass.ds(s, 1)], min_val=0, max_val=EXPERTS)
                        nc.scalar.activation(f_w[layer][q].rearrange("p (k n) -> p k n", n=HB),
                                             weff[:, layer * KH:(layer + 1) * KH, bass.ds(e, 1), :].rearrange("p k a n -> p k (a n)"),
                                             ACT.Copy).then_inc(w_copied[layer], 1)
            act.wait_ge(half_used, BLOCKS * HALVES)
            act.wait_ge(weff_made, LAYERS * KH * 2)
            pipeline(act, iteration)

        @block.vector
        def _(dve):
            V = nc.vector
            chain, tile = [0], [0]

            def stats_tile():
                t = tile[0]
                if t == KT:
                    return
                if t % 8 == 0:
                    dve.wait_ge(x_loaded[t // 8], 16)
                V.bn_stats(st6[:, t, :], xm[:, t, :]).then_inc(stats_made, 1)
                tile[0] += 1

            def link(ins):
                chain[0] += 1
                ins.then_inc(dve_step, 1)
                stats_tile()
                dve.wait_ge(dve_step, chain[0])

            dve.wait_ge(w_loaded, 32)
            link(V.tensor_reduce(w_mean[:, :], w_sb, AX_X, ALU.add))
            link(V.tensor_scalar(w_mean[:, :], w_mean[:, :], 1.0 / D, None, ALU.mult))
            V.tensor_tensor(bsc[:, 0:1], b_col[:, :], b_col[:, :], ALU.mult)
            V.tensor_scalar(w_sb, w_sb, w_mean[:, :], None, ALU.subtract).then_inc(w_centred, 1)

            dve.wait_ge(route_loaded, 32)
            link(V.tensor_copy(r_f[:, :], r_int[:, :]))
            link(V.tensor_scalar(valid[:, :], r_f[:, :], 0.0, None, ALU.is_ge))
            link(V.scalar_tensor_tensor(out=valid[:, :], in0=r_f[:, :], scalar=float(EXPERTS - 1), in1=valid[:, :],
                                        op0=ALU.is_le, op1=ALU.mult))
            link(V.scalar_tensor_tensor(out=r_f[:, :], in0=r_f[:, :], scalar=-float(EXPERTS), in1=valid[:, :],
                                        op0=ALU.add, op1=ALU.mult))
            link(V.tensor_scalar(r_f[:, :], r_f[:, :], float(EXPERTS), None, ALU.add))
            own = r_f[:, GROUPS:GROUPS + 1]
            dve.wait_ge(consts_made, 3)
            V.tensor_scalar(rt[1], r_f[:, 0:GROUPS], own, None, ALU.is_gt)
            link(V.tensor_scalar(rt[0], r_f[:, 0:GROUPS], own, None, ALU.is_equal))
            V.tensor_tensor(rt[2], rt[0], later, ALU.mult)
            link(V.tensor_tensor(rt[3], rt[0], earlier, ALU.mult))
            link(V.tensor_reduce(rc[:, 0:1], rt[3], AX_X, ALU.add))
            link(V.tensor_copy(rci[:, 0:1], rc[:, 0:1]))
            link(V.tensor_scalar(rci[:, 1:2], rci[:, 0:1], 1, None, ALU.bitwise_and))
            link(V.tensor_copy(rc[:, 1:2], rci[:, 1:2]))
            link(V.tensor_scalar(rc[:, 2:3], rc[:, 1:2], -1.0, 1.0, ALU.mult, ALU.add))
            V.tensor_tensor(rt[4], rt[1], rt[2], ALU.add).then_inc(even_ready, 1)
            for _ in range(10):
                stats_tile()
            dve.wait_ge(slot_mm, 1)
            link(V.tensor_tensor(rc[:, 3:4], bank[6][0:GROUPS, 511:512], rc[:, 1:2], ALU.subtract))
            V.tensor_scalar(lead[:, 0, :], iota_f[:, :], rc[:, 3:4], rc[:, 2:3], ALU.is_equal, ALU.mult)
            V.tensor_scalar(lead[:, 1, :], iota_f[:, :], rc[:, 3:4], rc[:, 1:2], ALU.is_equal, ALU.mult).then_inc(lead_ready, 1)
            for _ in range(4):
                stats_tile()
            dve.wait_ge(tables_mm, 1)
            link(V.tensor_copy(mrow[0:1, 0:5, :].rearrange("a k s -> a (k s)"), bank[6][0:1, 0:5 * SLOTS]))
            m = [mrow[0:1, k, :] for k in range(8)]
            link(V.tensor_scalar(m[4], m[4], -1.0, 1.0, ALU.mult, ALU.add))
            link(V.tensor_tensor(m[5], m[4], m[0], ALU.mult))
            link(V.tensor_tensor(m[5], m[5], m[3], ALU.add))
            link(V.tensor_scalar(m[1], m[1], -1.0, 1.0, ALU.mult, ALU.add))
            V.memset(trash[:, :, 0], float(TRASH))
            link(V.memset(trash[:, :, 1], float(TRASH + 2)))
            flat_trash = trash[:, :, :].rearrange("a s two -> a (s two)")
            V.tensor_tensor(m[6], m[1], flat_trash, ALU.mult)
            link(V.scalar_tensor_tensor(out=m[7], in0=flat_trash, scalar=1.0, in1=m[4], op0=ALU.add, op1=ALU.mult))
            V.tensor_tensor(m[6], m[6], m[0], ALU.add)
            link(V.tensor_tensor(m[7], m[7], m[3], ALU.add))
            for k, src in enumerate((0, 5, 2, 6, 7)):
                ins = V.tensor_copy(mint[0:1, k, :], m[src])
            ins.then_inc(meta_ready, 1)

            def inverse_root(dst, src, width, chained):
                ti, tf = tmp_i[:, 0:width], tmp_f[:, 0:width]
                chained(V.tensor_scalar(ti, src.bitcast(I32), 1, None, ALU.logical_shift_right))
                chained(V.tensor_scalar(dst.bitcast(I32), ti, -1.0, float(0x5F3759DF), ALU.mult, ALU.add))
                for _ in range(3):
                    chained(V.tensor_tensor(tf, dst, dst, ALU.mult))
                    chained(V.scalar_tensor_tensor(out=tf, in0=tf, scalar=-0.5, in1=src, op0=ALU.mult, op1=ALU.mult))
                    chained(V.scalar_tensor_tensor(out=dst, in0=tf, scalar=1.5, in1=dst, op0=ALU.add, op1=ALU.mult))

            while tile[0] < KT:
                stats_tile()
            dve.wait_ge(stats_made, KT)
            for t in range(KT):
                ins = V.bn_aggr(mv[:, t, :], st6[:, t, :])
            link(ins)

            def stt(o, a, s, b, op0, op1):
                return V.scalar_tensor_tensor(out=o, in0=a, scalar=s, in1=b, op0=op0, op1=op1)

            def artanh(o, a, ask, meanwhile=lambda: None):
                link(V.tensor_scalar(row[10], a, CLIP, None, ALU.min))
                V.tensor_scalar(row[11], row[10], 0.25, None, ALU.is_ge).then_inc(fn_asked, 1)
                link(V.tensor_tensor(row[16], row[10], row[10], ALU.mult))
                link(V.tensor_scalar(row[17], row[16], ATANH_SERIES[0], None, ALU.mult))
                for c in ATANH_SERIES[1:]:
                    link(stt(row[17], row[17], c, row[16], ALU.add, ALU.mult))
                link(stt(row[17], row[17], 1.0, row[10], ALU.add, ALU.mult))
                meanwhile()
                dve.wait_ge(fn_done, ask)
                link(V.tensor_tensor(row[12], row[12], row[13], ALU.subtract))
                link(stt(row[12], row[12], 0.5, row[17], ALU.mult, ALU.subtract))
                link(V.tensor_tensor(row[12], row[12], row[11], ALU.mult))
                link(V.tensor_tensor(o, row[12], row[17], ALU.add))

            def rows_of(first, count):
                return sc[:, first:first + count, :].rearrange("p a t -> p (a t)")

            def sum_squares(g):
                dve.wait_ge(mx_squared, g + 1)
                V.tensor_reduce(row[3][:, 4 * g:4 * g + 4], sq[:, g % 2, :].rearrange("p (t d) -> p t d", d=D),
                                AX_X, ALU.add).then_inc(squares_summed, 1)

            flat_sc = sc[:, :, :].rearrange("p n t -> p (n t)")
            dve.wait_ge(w_turned, 1)
            b_sq = bank[7][:, D + 1:D + 2]
            V.tensor_scalar(row[0], mv[:, :, 1], LN_EPS, None, ALU.add)
            V.tensor_scalar(row[1], mv[:, :, 1], float(D), MIN_SQ, ALU.mult, ALU.max)
            link(V.tensor_scalar(row[2][:, 0:1], b_sq, MIN_SQ, None, ALU.max))
            inverse_root(flat_sc[:, 4 * KT:6 * KT + 1], flat_sc[:, 0:2 * KT + 1], 2 * KT + 1, link)
            V.tensor_copy(bsc[:, 2:3], row[6][:, 0:1])
            V.tensor_tensor(row[7], row[1], row[5], ALU.mult)
            V.tensor_tensor(bsc[:, 1:2], row[2][:, 0:1], row[6][:, 0:1], ALU.mult).then_inc(bias_asked, 1)
            dve.wait_ge(bias_asked, 1)
            link(V.tensor_tensor(row[7], row[7], row[4], ALU.mult))
            for g in range(SQUARES_ON_ACT, QUADS - 2):
                sum_squares(g)
            artanh(row[19], row[7], 2, lambda: [sum_squares(g) for g in range(QUADS - 2, QUADS)])
            dve.wait_ge(squares_summed, QUADS - SQUARES_ON_ACT)
            link(V.tensor_scalar(row[2], row[3], MIN_SQ, None, ALU.max))
            inverse_root(row[6], row[2], KT, link)
            V.tensor_tensor(row[19], row[19], row[5], ALU.mult)
            link(V.tensor_tensor(row[14], row[2], row[6], ALU.mult))
            V.tensor_tensor(row[14], row[14], row[19], ALU.mult).then_inc(fn_asked, 1)
            dve.wait_ge(bias_tanh, 1)
            link(V.scalar_tensor_tensor(out=bsc[:, 4:5], in0=bsc[:, 3:4], scalar=MAX_NORM, in1=bsc[:, 2:3],
                                        op0=ALU.min, op1=ALU.mult))
            fac = bsc[:, 4:5]
            dve.wait_ge(mx_copied, 2 * QUADS)
            V.tensor_scalar(row[18], row[18], fac, None, ALU.mult)
            link(V.tensor_tensor(bsc[:, 5:6], fac, fac, ALU.mult))
            link(V.tensor_tensor(bsc[:, 5:6], bsc[:, 5:6], b_sq, ALU.mult))
            y2 = bsc[:, 5:6]
            dve.wait_ge(fn_done, 3)
            link(V.tensor_scalar(row[15], row[15], MAX_NORM, None, ALU.min))
            link(V.tensor_tensor(row[9], row[15], row[6], ALU.mult))
            link(V.tensor_tensor(row[15], row[15], row[15], ALU.mult))
            link(V.tensor_tensor(row[14], row[18], row[9], ALU.mult))
            link(V.tensor_scalar(row[14], row[14], 2.0, 1.0, ALU.mult, ALU.add))
            link(stt(row[16], row[15], y2, row[14], ALU.mult, ALU.add))
            link(V.tensor_scalar(row[16], row[16], MIN_NORM, None, ALU.max))
            link(V.reciprocal(row[16], row[16]))
            link(stt(row[14], row[14], y2, row[16], ALU.add, ALU.mult))
            link(V.tensor_tensor(row[20], row[14], row[9], ALU.mult))
            link(V.tensor_scalar(row[15], row[15], -1.0, 1.0, ALU.mult, ALU.add))
            link(V.tensor_tensor(row[21], row[15], row[16], ALU.mult))
            link(V.tensor_tensor(row[14], row[20], row[3], ALU.mult))
            link(stt(row[15], row[21], 2.0, row[18], ALU.mult, ALU.mult))
            link(V.tensor_tensor(row[14], row[14], row[15], ALU.add))
            link(V.tensor_tensor(row[14], row[14], row[20], ALU.mult))
            link(stt(row[15], row[21], y2, row[21], ALU.mult, ALU.mult))
            link(V.tensor_tensor(row[14], row[14], row[15], ALU.add))
            link(V.tensor_scalar(row[4], row[14], MIN_SQ, None, ALU.max))
            inverse_root(row[8], row[4], KT, link)
            link(V.tensor_tensor(row[6], row[4], row[8], ALU.mult))
            link(V.tensor_scalar(row[19], row[6], MAX_NORM, None, ALU.min))
            artanh(row[19], row[19], 5)
            link(V.tensor_tensor(row[19], row[19], row[8], ALU.mult))
            link(stt(row[21], row[21], fac, row[19], ALU.mult, ALU.mult))
            V.tensor_tensor(row[20], row[20], row[19], ALU.mult).then_inc(gains_ready, 1)

            def split_lo(b, c):
                if isinstance(b, int) and b == 0 and c < EARLY:
                    return
                if isinstance(b, int) and b == 0 and c == EARLY:
                    dve.wait_ge(lo_made, EARLY * SUBS)
                for h in range(SUBS):
                    at = (c * SUBS + h) % PART
                    dve.wait_ge(hi_made, b * HALVES + c * SUBS + h + 1)
                    V.tensor_tensor(adj_lo[:, at, :], raw_c[c % RAW][:, h * SW:(h + 1) * SW],
                                    adj_hi[:, at, :].bitcast(F32), ALU.subtract).then_inc(lo_made, 1)

            def sum_quad(g):
                if g == 0:
                    dve.wait_ge(wload, 16 * WLOADS)
                dve.wait_ge(mx_scaled, g + 1)
                for t in range(4 * g, 4 * g + 4):
                    ins = stt(xm[:, t, :], b_bc[:, :], row[21][:, t:t + 1], xm[:, t, :], ALU.mult, ALU.add)
                ins.then_inc(xt_sum, 1)

            LINKS = 6

            def post(b, par, step, positive=rl[:, :]):
                g = [ga[:, k, :] for k in range(16)]
                pair = [ga[:, k:k + 2, :].rearrange("p a q -> p (a q)") for k in range(0, 8, 2)]
                per_tile = lambda ap: ap.rearrange("p (q d) -> p q d", d=D)
                linked = [(0, 0, 5, 6)[step]]

                def chained(ins):
                    linked[0] += 1
                    ins.then_inc(ga_step, 1)
                    dve.wait_ge(ga_step, b * LINKS + linked[0])
                if step == 0:
                    wait(dve, ln_ready, b)
                    dve.wait_ge(rows_squared, b + 1)
                    V.tensor_reduce(g[0], per_tile(sq[:, 0, :]), AX_X, ALU.add).then_inc(sums_read, 1)
                    dve.wait_ge(relu_squared, b + 1)
                    V.tensor_reduce(g[1], per_tile(sq[:, 1, :]), AX_X, ALU.add).then_inc(sums_read, 1)
                    dve.wait_ge(sums_read, 2 * b + 2)
                    V.tensor_scalar(pair[1], pair[0], MIN_SQ, None, ALU.max).then_inc(norms_asked, 1)
                if step == 1:
                    dve.wait_ge(norms_rooted, b + 1)
                    chained(V.tensor_tensor(pair[3], pair[1], pair[2], ALU.mult))
                    chained(stt(g[8], g[6], ATANH_MAX, g[4], ALU.min, ALU.mult))
                    chained(V.tensor_tensor(g[9], g[7], g[8], ALU.mult))
                    chained(V.tensor_scalar(g[10], g[9], MIN_NORM, None, ALU.max))
                    V.reciprocal(g[12], g[10]).then_inc(tanh_asked, 1)
                    dve.wait_ge(tanh_asked, b + 1)
                    chained(V.tensor_tensor(g[13], g[8], g[12], ALU.mult))
                if step == 2:
                    dve.wait_ge(tanh_made, b + 1)
                    chained(stt(g[14], g[11], MAX_NORM, g[13], ALU.min, ALU.mult))
                    dve.wait_ge(xr_loaded[par], (b // 2 + 1) * 16 if isinstance(b, int) else (b - par) * 8 + 16)
                    for q in range(TILES):
                        V.scalar_tensor_tensor(out=xr[:, par, q, :], in0=positive[:, q * D:(q + 1) * D], scalar=ga[:, 14, q:q + 1],
                                               in1=xr[:, par, q, :], op0=ALU.mult, op1=ALU.add).then_inc(x2_ready, 1)
                    for q in range(TILES):
                        dve.wait_ge(x2_ready, b * TILES + q + 1)
                        ins = V.bn_stats(st6_b[:, q, :], xr[:, par, q, :])
                    ins.then_inc(stats_b, 1)
                    dve.wait_ge(stats_b, b + 1)
                if step == 3:
                    for q in range(TILES):
                        ins = V.bn_aggr(mv_b[:, q, :], st6_b[:, q, :])
                    ins.then_inc(mean_b, 1)
                    dve.wait_ge(mean_b, b + 1)
                    V.tensor_scalar(var_b[:, :, 0], mv_b[:, :, 1], LN_EPS, None, ALU.add).then_inc(var_ready, 1)

            def block_step(b, par):
                first = isinstance(b, int) and b == 0
                for c in range(CHUNKS):
                    if first:
                        if c == 0:
                            sum_quad(0)
                        if c + 1 < CHUNKS:
                            sum_quad(c + 1)
                    split_lo(b, c)
                    if not first and c in DVE_POST_AT:
                        post(b - 1, 1 - par, DVE_POST_AT.index(c))
            blocks(dve, block_step)
            for step in range(4):
                post(BLOCKS - 1, 1, step, work[:, 0, :])
            dve.wait_ge(turned, 2 * BLOCKS - 2)
            dve.wait_ge(rstd_ready, BLOCKS)
            for q in range(TILES):
                ins = V.tensor_scalar(rl[:, q * D:(q + 1) * D], xr[:, 1, q, :], mv_b[:, q, 0:1], rstd_b[:, q, :],
                                      ALU.subtract, ALU.mult)
            ins.then_inc(ln_ready, 1)

            def relu_bias(layer, q, bank_n, dst, made):
                for k in range(KH):
                    at = k * HB + HID
                    V.tensor_scalar(dst[:, k * P:(k + 1) * P], bank[bank_n][:, k * P:(k + 1) * P],
                                    f_w[layer][q][:, at:at + 1], 0.0, ALU.add, ALU.max).then_inc(made, 1)

            def iteration(i, par):
                if live(i - WO):
                    at = [dve.value_load(mint[0:1, 3 + g, bass.ds(i - WO, 1)], min_val=0, max_val=TRASH + 3) for g in range(2)]
                s, q = i - L1, par
                if live(s):
                    dve.wait_ge(l1_done, s + 1)
                    relu_bias(1, q, 4 * q + 2, f_h2[q], h2_made)
                s, q = i - L0, 1 - par
                if live(s):
                    dve.wait_ge(l0_done, s + 1)
                    relu_bias(0, q, 4 * q + 1, f_h1[q], h1_made)
                s, q = i - WO, 1 - par
                if live(s):
                    dve.wait_ge(wo_done, s + 1)
                    wait(dve, o_stored[q], (s - q) * 16)
                    for g in range(2):
                        group = raw[:, bass.ds(at[g] * GR, GR)]
                        V.scalar_tensor_tensor(out=group, in0=bank[4 * q + 3][:, g * GR:(g + 1) * GR], scalar=bo_col[:, :],
                                               in1=group, op0=ALU.add, op1=ALU.add).then_inc(o_made, 1)
            dve.wait_ge(weff_made, LAYERS * KH * 2)
            dve.wait_ge(meta_ready, 1)
            dve.wait_ge(x2t_loaded, 16)
            dve.wait_ge(turned_copied, 2 * BLOCKS)
            dve.wait_ge(trash_made, 1)
            pipeline(dve, iteration)

        @block.tensor
        def _(pe):
            T = nc.tensor
            pe.wait_ge(consts_made, 3)

            def keep_warm(count):
                for _ in range(count):
                    T.matmul(bank[5][:, 0:P], ident[:, :], ones[:, :], start=True, stop=True)

            pe.wait_ge(w_centred, 1)
            T.transpose(bank[7][:, 0:D], w_sb, ident[:, :])
            T.matmul(bank[7][:, D:D + 1], w_sb, b_col[:, :], start=True, stop=True)
            T.matmul(bank[7][:, D + 1:D + 2], ones[:, :], bsc[:, 0:1], start=True, stop=True).then_inc(w_turned, 1)

            def transpose_quad(g):
                pe.wait_ge(x_loaded[g // 2], 16)
                if g >= 2:
                    pe.wait_ge(x_turned, g - 1)
                for q in range(4):
                    mm = T.transpose(bank[g % 2][:, q * P:(q + 1) * P], xm[:, 4 * g + q, :], ident[:, :])
                mm.then_inc(x_in_psum, 1)

            transpose_quad(0)
            pe.wait_ge(wt_ready, 1)
            for g in range(QUADS):
                if g + 1 < QUADS:
                    transpose_quad(g + 1)
                pe.wait_ge(x_turned, g + 1)
                if g >= 2:
                    pe.wait_ge(mx_squared, g - 1)
                for q in range(4):
                    mm = T.matmul(mx_pair[g % 2][:, q // 2, q % 2, :], work[:, g % 2, q * P:(q + 1) * P], wt_sb,
                                  start=True, stop=True)
                mm.then_inc(mx_in_psum, 1)
                if g == 1:
                    pe.wait_ge(even_ready, 1)
                    T.matmul(bank[6][0:GROUPS, 511:512], rt[4], rc[:, 2:3], start=True, stop=True).then_inc(slot_mm, 1)
                if g == 2:
                    pe.wait_ge(lead_ready, 1)
                    for k, (col, h) in enumerate(((rc[:, 7:8], 0), (ones[0:GROUPS, 0:1], 0), (r_f[:, GROUPS:GROUPS + 1], 0),
                                                  (rc[:, 7:8], 1), (ones[0:GROUPS, 0:1], 1))):
                        mm = T.matmul(bank[6][0:1, k * SLOTS:(k + 1) * SLOTS], col, lead[:, h, :], start=True, stop=True)
                    mm.then_inc(tables_mm, 1)

            def rows_of_block(b, par):
                pe.wait_ge(support_copied, b + 1)
                wait(pe, relu_made, b - 1)
                for q in range(TILES):
                    mm = T.transpose(bank[2 + par][:, q * P:(q + 1) * P], work[:, par, q * P:(q + 1) * P], ident[:, :])
                mm.then_inc(rows_ready, 1)

            def turn(b, par):
                pe.wait_ge(ln_ready, b + 1)
                wait(pe, turned_copied, 2 * b)
                for q in range(TILES):
                    mm = T.transpose(bank[4][:, q * P:(q + 1) * P], rl[:, q * P:(q + 1) * P], ident[:, :])
                mm.then_inc(turned, 1)
                for q in range(TILES):
                    mm = T.transpose(bank[6][:, q * P:(q + 1) * P], xr[:, par, q, :], ident[:, :])
                mm.then_inc(turned, 1)

            def block_step(b, par):
                first = isinstance(b, int) and b == 0
                wait(pe, support_copied, b - 1)
                for c in range(CHUNKS):
                    if first:
                        pe.wait_ge(xt_ready, c + 1)
                    for k in range(CK):
                        t = c * CK + k
                        half, k_in = c * SUBS + k // SK, k % SK
                        if k_in == 0:
                            pe.wait_ge(lo_made, b * HALVES + half + 1)
                        hi = adj_hi[:, half % PART, k_in * ROWS:(k_in + 1) * ROWS]
                        lo = adj_lo[:, half % PART, k_in * ROWS:(k_in + 1) * ROWS]
                        T.matmul(bank[par][:, :], xt_hi[:, t, :], hi, start=(t == 0), stop=False)
                        T.matmul(bank[par][:, :], xt_hi[:, t, :], lo, start=False, stop=False)
                        mm = T.matmul(bank[par][:, :], xt_lo[:, t, :], hi, start=False, stop=(t == KT - 1))
                        if k_in == SK - 1:
                            mm.then_inc(half_used, 1)
                    if c == CHUNKS - 1:
                        T.matmul(bank[5][:, 0:1], ident[:, :], ones[:, 0:1], start=True, stop=True).then_inc(support_ready, 1)
                    if not first and c == 2:
                        rows_of_block(b - 1, 1 - par)
                    if c == 0 and not (isinstance(b, int) and b < 2):
                        turn(b - 2, par)
            pe.wait_ge(gains_ready, 1)
            keep_warm(9)
            blocks(pe, block_step, peeled=4)
            rows_of_block(BLOCKS - 1, 1)
            turn(BLOCKS - 2, 0)
            pe.wait_ge(x2_ready, BLOCKS * TILES)
            keep_warm(9)
            turn(BLOCKS - 1, 1)

            def routed(w, h, sums, done):
                for m in range(KH):
                    for k in range(KH):
                        mm = T.matmul(sums[:, m * P:(m + 1) * P], w[:, k * HB + m * P:k * HB + (m + 1) * P],
                                      h[:, k * P:(k + 1) * P], start=(k == 0), stop=(k == KH - 1))
                mm.then_inc(done, 1)

            def iteration(i, par):
                s, q = i - WO, 1 - par
                if live(s):
                    pe.wait_ge(h2_made, KH * s + KH)
                    wait(pe, o_made, 2 * s - 2)
                    for k in range(KH):
                        mm = T.matmul(bank[4 * q + 3][:, 0:P], wo_sb[:, k, :], f_h2[q][:, k * P:(k + 1) * P],
                                      start=(k == 0), stop=(k == KH - 1))
                    mm.then_inc(wo_done, 1)
                s, q = i - L1, par
                if live(s):
                    pe.wait_ge(h1_made, KH * s + KH)
                    pe.wait_ge(w_copied[1], s + 1)
                    routed(f_w[1][q], f_h1[q], bank[4 * q + 2], l1_done)
                s, q = i - L0, 1 - par
                if live(s):
                    pe.wait_ge(h0_made, KH * s + KH)
                    pe.wait_ge(w_copied[0], s + 1)
                    routed(f_w[0][q], f_h0[q], bank[4 * q + 1], l0_done)
                s, q = i - WI, par
                if live(s):
                    pe.wait_ge(gathered, 2 * s + 2)
                    for k in range(KH):
                        mm = T.matmul(bank[4 * q][:, k * P:(k + 1) * P], wi_sb[:, k * P:(k + 1) * P], f_xt[q],
                                      start=True, stop=True)
                    mm.then_inc(wi_done, 1)
            pe.wait_ge(meta_ready, 1)
            pe.wait_ge(weff_made, LAYERS * KH * 2)
            pe.wait_ge(turned_copied, 2 * BLOCKS - 1)
            pipeline(pe, iteration)


def kernel(**inputs):
    import concourse.bacc as bacc
    from concourse.bass_utils import run_bass_kernel_spmd as run

    nc = bacc.Bacc("TRN2", target_bir_lowering=False, num_devices=1)
    arrays = {}

    def dram(name, a):
        a = np.ascontiguousarray(a)
        arrays[name] = a
        return nc.dram_tensor(name, a.shape, mybir.dt.from_np(a.dtype), kind="ExternalInput").ap()

    def get(name):
        return np.asarray(inputs[name])

    def by_partition(a):
        n = a.shape[1]
        a = a.transpose(0, 3, 1, 2).reshape(LAYERS, KH, P, n, HID)
        return a.transpose(2, 0, 1, 3, 4).reshape(P, LAYERS * KH, n, HID)

    def bias_by_partition(a):
        n = a.shape[1]
        return a.reshape(LAYERS, n, KH, P).transpose(3, 0, 2, 1).reshape(P, LAYERS * KH, n)

    def with_bias(weights, biases):
        return np.concatenate([by_partition(get(weights)), bias_by_partition(get(biases))[..., None]], axis=3)

    args = [
        dram("x", get("x")),
        dram("adj_t", get("adj").reshape(BLOCKS, ROWS, P, KT).transpose(0, 2, 3, 1).reshape(BLOCKS, P, KT * ROWS)),
        dram("w", get("L0_gnn_weight")),
        dram("bias", get("L0_gnn_bias")),
        dram("route", get("L0_ffn_route_id")),
        dram("wi_t", get("L0_ffn_Wi").T),
        dram("bi", get("L0_ffn_bi").reshape(KH, P).T),
        dram("wr_t", with_bias("L0_ffn_Wr", "L0_ffn_br")),
        dram("ws_t", with_bias("L0_ffn_Ws", "L0_ffn_bs")[:, :, 0, :]),
        dram("wo_t", get("L0_ffn_Wo").T.reshape(KH, P, D).transpose(1, 0, 2)),
        dram("bo", get("L0_ffn_bo")),
        nc.dram_tensor("x2t_dram", (D, N), F32, kind="Internal").ap(),
        nc.dram_tensor("out_t", (GROUPS + 4, D, GR), F32, kind="ExternalOutput").ap(),
    ]
    build(nc, *args)
    r = run(nc, [arrays], core_ids=[0])
    return r.results[0]["out_t"][:GROUPS].transpose(0, 2, 1).reshape(N, D)
```
